# Optimizing a Trainium2 kernel written in Bass

```python
import numpy as np
import jax
import jax.numpy as jnp

def _softmax(x, axis=-1):
    return jax.nn.softmax(x, axis=axis)

def _gelu(x):
    return jax.nn.gelu(x, approximate=True)

def _silu(x):
    return jax.nn.silu(x)

def _sigmoid(x):
    return jax.nn.sigmoid(x)

def _layernorm(x, axis=-1, eps=1e-05):
    m = jnp.mean(x, axis=axis, keepdims=True)
    v = jnp.var(x, axis=axis, keepdims=True)
    return (x - m) / jnp.sqrt(v + eps)

def _scatter_add(tgt, idx, src, axis=0):
    return tgt.at[idx].add(src)

def _segment_sum(src, seg, n):
    return jax.ops.segment_sum(src, seg, n)
kernel_name = 'mk_cond_seq_d2_seqx_r4_8cc434'

def setup_inputs(seed: int=0):
    np.random.seed(seed)
    _w = jnp.asarray

    def _rec_inputs():
        import jax
        import jax.numpy as jnp
        _rk = jax.random.key(seed)
        x = -0.0002928 + 1 * jax.random.normal(jax.random.fold_in(_rk, 1), (2, 1024, 256), jnp.float32)
        _lenS = 1024 - jax.random.randint(jax.random.fold_in(_rk, 7), (2,), 0, max(1, 1024 // 4) + 1, jnp.int32)
        _lenS2 = 1024 - jax.random.randint(jax.random.fold_in(_rk, 8), (2,), 0, max(1, 1024 // 4) + 1, jnp.int32)
        cond_1024 = 0.000887014 + 1.03683 * jax.random.normal(jax.random.fold_in(_rk, 11), (2, 256), jnp.float32)
        _validS = jnp.arange(1024)[None, :] < _lenS[:, None]
        _validS2 = jnp.arange(1024)[None, :] < _lenS2[:, None]
        _causal = jnp.tril(jnp.ones((1024, 1024), dtype=bool))
        mask_BxS_ik0 = jnp.where(jnp.broadcast_to(_validS[:, :], (2, 1024)), 0, 1).astype(jnp.int32)
        return (x, cond_1024, mask_BxS_ik0)
    x, cond_1024, mask_BxS_ik0 = _rec_inputs()

    def _L0_cond_setup():
        import jax, jax.numpy as jnp
        import numpy as np
        B, L, D_MODEL, COND = (2, 512, 256, 256)
        D_STATE, EXPAND = (64, 2)
        D_INNER = EXPAND * D_MODEL
        MLP_H = 2 * D_MODEL
        EPS = 1e-05

        def _adaln(x, c, w, b):
            mod = (c @ w + b)[:, None, :]
            shift, scale, gate = jnp.split(mod, 3, axis=-1)
            mu = jnp.mean(x, axis=-1, keepdims=True)
            var = jnp.var(x, axis=-1, keepdims=True)
            normed = (x - mu) * jax.lax.rsqrt(var + EPS) * (1.0 + scale) + shift
            return (normed, gate)

        def _ssm(h, in_w, xproj_w, dt_bias, A_log, Dskip, out_w):
            xz = h @ in_w
            xs, z = jnp.split(xz, 2, axis=-1)
            xs = jax.nn.silu(xs)
            proj = xs @ xproj_w
            dt = jax.nn.softplus(proj[..., :D_INNER] + dt_bias)
            Bm = proj[..., D_INNER:D_INNER + D_STATE]
            Cm = proj[..., D_INNER + D_STATE:]
            A = -jnp.exp(A_log)

            def step(hst, ins):
                dt_t, B_t, C_t, x_t = ins
                dA = jnp.exp(dt_t[:, :, None] * A)
                hst = hst * dA + (dt_t * x_t)[:, :, None] * B_t[:, None, :]
                y_t = jnp.einsum('bds,bs->bd', hst, C_t)
                return (hst, y_t)
            tm = lambda a: jnp.swapaxes(a, 0, 1)
            h0 = jnp.zeros((h.shape[0], D_INNER, D_STATE), h.dtype)
            _, ys = jax.lax.scan(step, h0, (tm(dt), tm(Bm), tm(Cm), tm(xs)))
            y = jnp.swapaxes(ys, 0, 1) + xs * Dskip
            return y * jax.nn.silu(z) @ out_w
        key = jax.random.key(seed)
        ks = jax.random.split(key, 24)
        p = lambda i, shape, s=0.02: jax.random.normal(ks[i], shape, jnp.float32) * s
        inp = {'x': jax.random.normal(ks[0], (B, L, D_MODEL), jnp.float32), 'c': jax.random.normal(ks[1], (B, COND), jnp.float32), 'adaln_mamba_w': p(2, (COND, 3 * D_MODEL)), 'adaln_mamba_b': jnp.zeros((3 * D_MODEL,), jnp.float32), 'adaln_mlp_w': p(3, (COND, 3 * D_MODEL)), 'adaln_mlp_b': jnp.zeros((3 * D_MODEL,), jnp.float32), 'mlp_w1': p(4, (D_MODEL, MLP_H)), 'mlp_w2': p(5, (D_MODEL, MLP_H)), 'mlp_w3': p(6, (MLP_H, D_MODEL))}
        a_init = jnp.log(jnp.tile(jnp.arange(1, D_STATE + 1, dtype=jnp.float32), (D_INNER, 1)))
        for j, pre in enumerate(['fwd', 'bwd']):
            o = 7 + 6 * j
            inp[f'{pre}_in_w'] = p(o, (D_MODEL, 2 * D_INNER))
            inp[f'{pre}_xproj_w'] = p(o + 1, (D_INNER, D_INNER + 2 * D_STATE))
            inp[f'{pre}_dt_bias'] = jnp.zeros((D_INNER,), jnp.float32)
            inp[f'{pre}_A_log'] = a_init
            inp[f'{pre}_D'] = jnp.ones((D_INNER,), jnp.float32)
            inp[f'{pre}_out_w'] = p(o + 2, (D_INNER, D_MODEL))
        return inp
    _L0_cond_all = _L0_cond_setup()
    _L0_cond_in = {k: v for k, v in _L0_cond_all.items() if k in ('adaln_mamba_w', 'adaln_mamba_b', 'adaln_mlp_w', 'adaln_mlp_b', 'mlp_w1', 'mlp_w2', 'mlp_w3', 'fwd_in_w', 'fwd_xproj_w', 'fwd_dt_bias', 'fwd_A_log', 'fwd_D', 'fwd_out_w', 'bwd_in_w', 'bwd_xproj_w', 'bwd_dt_bias', 'bwd_A_log', 'bwd_D', 'bwd_out_w')}
    del _L0_cond_all

    def _L1_cond_setup():
        import jax, jax.numpy as jnp
        import numpy as np
        EMBED = 256
        HEADS = 16
        HEAD_DIM = EMBED // HEADS
        MLP = 4 * EMBED
        EPS = 1e-06

        def _adaln(x, c, norm_w, scale_w, scale_b, shift_w, shift_b):
            sc = jax.nn.silu(c)
            shift = sc @ shift_w.T + shift_b
            scale = jnp.clip(sc @ scale_w.T + scale_b + 1.0, 0.1, 10.0)
            norm = jnp.maximum(jnp.linalg.norm(x, axis=-1, keepdims=True) * x.shape[-1] ** (-0.5), EPS)
            h = x / norm * norm_w
            return h * scale[:, None, :] + shift[:, None, :]

        def _attention(x, attention_mask, qkv_w, proj_w, proj_b):
            B, N, C = x.shape
            qkv = (x @ qkv_w.T).reshape(B, N, 3, HEADS, HEAD_DIM)
            q = qkv[:, :, 0].transpose(0, 2, 1, 3)
            k = qkv[:, :, 1].transpose(0, 2, 1, 3)
            v = qkv[:, :, 2].transpose(0, 2, 1, 3)
            attn = jnp.einsum('bhnd,bhmd->bhnm', q, k) * HEAD_DIM ** (-0.5)
            mask = attention_mask[:, None, None, :]
            attn = jnp.where(mask == 0, -jnp.inf, attn)
            all_inf = jnp.all(attn == -jnp.inf, axis=-1, keepdims=True)
            attn = jnp.where(all_inf, 0.0, attn)
            p = jax.nn.softmax(attn, axis=-1)
            out = jnp.einsum('bhnm,bhmd->bhnd', p, v).transpose(0, 2, 1, 3).reshape(B, N, C)
            return out @ proj_w.T + proj_b

        def _mlp(x, w1, b1, w2, b2):
            h = x @ w1.T + b1
            x1, x2 = jnp.split(h, 2, axis=-1)
            return jax.nn.silu(x1) * x2 @ w2.T + b2
        key = jax.random.key(seed)
        ks = jax.random.split(key, 16)
        B, N, C = (2, 512, EMBED)
        x = jax.random.normal(ks[0], (B, N, C), dtype=jnp.float32)
        c = jax.random.normal(ks[1], (B, C), dtype=jnp.float32)
        attention_mask = jax.random.randint(ks[2], (B, N), 0, 2, dtype=jnp.int32)
        s = 0.02
        params = {'norm_w': jnp.ones((C,), jnp.float32), 'scale_w': s * jax.random.normal(ks[3], (C, C), jnp.float32), 'scale_b': s * jax.random.normal(ks[4], (C,), jnp.float32), 'shift_w': s * jax.random.normal(ks[5], (C, C), jnp.float32), 'shift_b': s * jax.random.normal(ks[6], (C,), jnp.float32), 'qkv_w': s * jax.random.normal(ks[7], (3 * C, C), jnp.float32), 'proj_w': s * jax.random.normal(ks[8], (C, C), jnp.float32), 'proj_b': s * jax.random.normal(ks[9], (C,), jnp.float32), 'mlp_w1': s * jax.random.normal(ks[10], (2 * MLP, C), jnp.float32), 'mlp_b1': s * jax.random.normal(ks[11], (2 * MLP,), jnp.float32), 'mlp_w2': s * jax.random.normal(ks[12], (C, MLP), jnp.float32), 'mlp_b2': s * jax.random.normal(ks[13], (C,), jnp.float32)}
        return {'x': x, 'c': c, 'attention_mask': attention_mask, **params}
    _L1_cond_all = _L1_cond_setup()
    _L1_cond_in = {k: v for k, v in _L1_cond_all.items() if k in ('norm_w', 'scale_w', 'scale_b', 'shift_w', 'shift_b', 'qkv_w', 'proj_w', 'proj_b', 'mlp_w1', 'mlp_b1', 'mlp_w2', 'mlp_b2')}
    del _L1_cond_all
    return {'x': x, 'cond_1024': cond_1024, 'mask_BxS_ik0': mask_BxS_ik0, 'L0_cond_adaln_mamba_w': _L0_cond_in['adaln_mamba_w'], 'L0_cond_adaln_mamba_b': _L0_cond_in['adaln_mamba_b'], 'L0_cond_adaln_mlp_w': _L0_cond_in['adaln_mlp_w'], 'L0_cond_adaln_mlp_b': _L0_cond_in['adaln_mlp_b'], 'L0_cond_mlp_w1': _L0_cond_in['mlp_w1'], 'L0_cond_mlp_w2': _L0_cond_in['mlp_w2'], 'L0_cond_mlp_w3': _L0_cond_in['mlp_w3'], 'L0_cond_fwd_in_w': _L0_cond_in['fwd_in_w'], 'L0_cond_fwd_xproj_w': _L0_cond_in['fwd_xproj_w'], 'L0_cond_fwd_dt_bias': _L0_cond_in['fwd_dt_bias'], 'L0_cond_fwd_A_log': _L0_cond_in['fwd_A_log'], 'L0_cond_fwd_D': _L0_cond_in['fwd_D'], 'L0_cond_fwd_out_w': _L0_cond_in['fwd_out_w'], 'L0_cond_bwd_in_w': _L0_cond_in['bwd_in_w'], 'L0_cond_bwd_xproj_w': _L0_cond_in['bwd_xproj_w'], 'L0_cond_bwd_dt_bias': _L0_cond_in['bwd_dt_bias'], 'L0_cond_bwd_A_log': _L0_cond_in['bwd_A_log'], 'L0_cond_bwd_D': _L0_cond_in['bwd_D'], 'L0_cond_bwd_out_w': _L0_cond_in['bwd_out_w'], 'L1_cond_norm_w': _L1_cond_in['norm_w'], 'L1_cond_scale_w': _L1_cond_in['scale_w'], 'L1_cond_scale_b': _L1_cond_in['scale_b'], 'L1_cond_shift_w': _L1_cond_in['shift_w'], 'L1_cond_shift_b': _L1_cond_in['shift_b'], 'L1_cond_qkv_w': _L1_cond_in['qkv_w'], 'L1_cond_proj_w': _L1_cond_in['proj_w'], 'L1_cond_proj_b': _L1_cond_in['proj_b'], 'L1_cond_mlp_w1': _L1_cond_in['mlp_w1'], 'L1_cond_mlp_b1': _L1_cond_in['mlp_b1'], 'L1_cond_mlp_w2': _L1_cond_in['mlp_w2'], 'L1_cond_mlp_b2': _L1_cond_in['mlp_b2']}

def reference(x, cond_1024, mask_BxS_ik0, L0_cond_adaln_mamba_w, L0_cond_adaln_mamba_b, L0_cond_adaln_mlp_w, L0_cond_adaln_mlp_b, L0_cond_mlp_w1, L0_cond_mlp_w2, L0_cond_mlp_w3, L0_cond_fwd_in_w, L0_cond_fwd_xproj_w, L0_cond_fwd_dt_bias, L0_cond_fwd_A_log, L0_cond_fwd_D, L0_cond_fwd_out_w, L0_cond_bwd_in_w, L0_cond_bwd_xproj_w, L0_cond_bwd_dt_bias, L0_cond_bwd_A_log, L0_cond_bwd_D, L0_cond_bwd_out_w, L1_cond_norm_w, L1_cond_scale_w, L1_cond_scale_b, L1_cond_shift_w, L1_cond_shift_b, L1_cond_qkv_w, L1_cond_proj_w, L1_cond_proj_b, L1_cond_mlp_w1, L1_cond_mlp_b1, L1_cond_mlp_w2, L1_cond_mlp_b2):
    import jax
    import jax.numpy as jnp

    def _L0_cond_ref(x, c, adaln_mamba_w, adaln_mamba_b, adaln_mlp_w, adaln_mlp_b, mlp_w1, mlp_w2, mlp_w3, fwd_in_w, fwd_xproj_w, fwd_dt_bias, fwd_A_log, fwd_D, fwd_out_w, bwd_in_w, bwd_xproj_w, bwd_dt_bias, bwd_A_log, bwd_D, bwd_out_w):
        import jax, jax.numpy as jnp
        import numpy as np
        B, L, D_MODEL, COND = (2, 512, 256, 256)
        D_STATE, EXPAND = (64, 2)
        D_INNER = EXPAND * D_MODEL
        MLP_H = 2 * D_MODEL
        EPS = 1e-05

        def _adaln(x, c, w, b):
            mod = (c @ w + b)[:, None, :]
            shift, scale, gate = jnp.split(mod, 3, axis=-1)
            mu = jnp.mean(x, axis=-1, keepdims=True)
            var = jnp.var(x, axis=-1, keepdims=True)
            normed = (x - mu) * jax.lax.rsqrt(var + EPS) * (1.0 + scale) + shift
            return (normed, gate)

        def _ssm(h, in_w, xproj_w, dt_bias, A_log, Dskip, out_w):
            xz = h @ in_w
            xs, z = jnp.split(xz, 2, axis=-1)
            xs = jax.nn.silu(xs)
            proj = xs @ xproj_w
            dt = jax.nn.softplus(proj[..., :D_INNER] + dt_bias)
            Bm = proj[..., D_INNER:D_INNER + D_STATE]
            Cm = proj[..., D_INNER + D_STATE:]
            A = -jnp.exp(A_log)

            def step(hst, ins):
                dt_t, B_t, C_t, x_t = ins
                dA = jnp.exp(dt_t[:, :, None] * A)
                hst = hst * dA + (dt_t * x_t)[:, :, None] * B_t[:, None, :]
                y_t = jnp.einsum('bds,bs->bd', hst, C_t)
                return (hst, y_t)
            tm = lambda a: jnp.swapaxes(a, 0, 1)
            h0 = jnp.zeros((h.shape[0], D_INNER, D_STATE), h.dtype)
            _, ys = jax.lax.scan(step, h0, (tm(dt), tm(Bm), tm(Cm), tm(xs)))
            y = jnp.swapaxes(ys, 0, 1) + xs * Dskip
            return y * jax.nn.silu(z) @ out_w
        h, gate = _adaln(x, c, adaln_mamba_w, adaln_mamba_b)
        h_fwd = _ssm(h, fwd_in_w, fwd_xproj_w, fwd_dt_bias, fwd_A_log, fwd_D, fwd_out_w)
        h_bwd = jnp.flip(_ssm(jnp.flip(h, 1), bwd_in_w, bwd_xproj_w, bwd_dt_bias, bwd_A_log, bwd_D, bwd_out_w), 1)
        x = x + gate * (h_fwd + h_bwd)
        h, gate = _adaln(x, c, adaln_mlp_w, adaln_mlp_b)
        mlp_out = jax.nn.silu(h @ mlp_w1) * (h @ mlp_w2) @ mlp_w3
        return x + gate * mlp_out

    def _L1_cond_ref(x, c, attention_mask, norm_w, scale_w, scale_b, shift_w, shift_b, qkv_w, proj_w, proj_b, mlp_w1, mlp_b1, mlp_w2, mlp_b2):
        import jax, jax.numpy as jnp
        import numpy as np
        EMBED = 256
        HEADS = 16
        HEAD_DIM = EMBED // HEADS
        MLP = 4 * EMBED
        EPS = 1e-06

        def _adaln(x, c, norm_w, scale_w, scale_b, shift_w, shift_b):
            sc = jax.nn.silu(c)
            shift = sc @ shift_w.T + shift_b
            scale = jnp.clip(sc @ scale_w.T + scale_b + 1.0, 0.1, 10.0)
            norm = jnp.maximum(jnp.linalg.norm(x, axis=-1, keepdims=True) * x.shape[-1] ** (-0.5), EPS)
            h = x / norm * norm_w
            return h * scale[:, None, :] + shift[:, None, :]

        def _attention(x, attention_mask, qkv_w, proj_w, proj_b):
            B, N, C = x.shape
            qkv = (x @ qkv_w.T).reshape(B, N, 3, HEADS, HEAD_DIM)
            q = qkv[:, :, 0].transpose(0, 2, 1, 3)
            k = qkv[:, :, 1].transpose(0, 2, 1, 3)
            v = qkv[:, :, 2].transpose(0, 2, 1, 3)
            attn = jnp.einsum('bhnd,bhmd->bhnm', q, k) * HEAD_DIM ** (-0.5)
            mask = attention_mask[:, None, None, :]
            attn = jnp.where(mask == 0, -jnp.inf, attn)
            all_inf = jnp.all(attn == -jnp.inf, axis=-1, keepdims=True)
            attn = jnp.where(all_inf, 0.0, attn)
            p = jax.nn.softmax(attn, axis=-1)
            out = jnp.einsum('bhnm,bhmd->bhnd', p, v).transpose(0, 2, 1, 3).reshape(B, N, C)
            return out @ proj_w.T + proj_b

        def _mlp(x, w1, b1, w2, b2):
            h = x @ w1.T + b1
            x1, x2 = jnp.split(h, 2, axis=-1)
            return jax.nn.silu(x1) * x2 @ w2.T + b2
        x = x + _attention(_adaln(x, c, norm_w, scale_w, scale_b, shift_w, shift_b), attention_mask, qkv_w, proj_w, proj_b)
        x = x + _mlp(_adaln(x, c, norm_w, scale_w, scale_b, shift_w, shift_b), mlp_w1, mlp_b1, mlp_w2, mlp_b2)
        return x
    x = _L0_cond_ref(x, cond_1024, L0_cond_adaln_mamba_w, L0_cond_adaln_mamba_b, L0_cond_adaln_mlp_w, L0_cond_adaln_mlp_b, L0_cond_mlp_w1, L0_cond_mlp_w2, L0_cond_mlp_w3, L0_cond_fwd_in_w, L0_cond_fwd_xproj_w, L0_cond_fwd_dt_bias, L0_cond_fwd_A_log, L0_cond_fwd_D, L0_cond_fwd_out_w, L0_cond_bwd_in_w, L0_cond_bwd_xproj_w, L0_cond_bwd_dt_bias, L0_cond_bwd_A_log, L0_cond_bwd_D, L0_cond_bwd_out_w)
    x = _L1_cond_ref(x, cond_1024, mask_BxS_ik0, L1_cond_norm_w, L1_cond_scale_w, L1_cond_scale_b, L1_cond_shift_w, L1_cond_shift_b, L1_cond_qkv_w, L1_cond_proj_w, L1_cond_proj_b, L1_cond_mlp_w1, L1_cond_mlp_b1, L1_cond_mlp_w2, L1_cond_mlp_b2)
    return x

_drawn_inputs = setup_inputs


def setup_inputs(seed=0):
    import zlib

    import numpy as np

    out = dict(_drawn_inputs(seed))
    spreads = {'L0_cond_adaln_mamba_b': (0.0, 0.1),
     'L0_cond_adaln_mlp_b': (0.0, 0.1),
     'L0_cond_fwd_dt_bias': (0.0, 0.1),
     'L0_cond_fwd_D': (1.0, 0.2),
     'L0_cond_bwd_dt_bias': (0.0, 0.1),
     'L0_cond_bwd_D': (1.0, 0.2),
     'L1_cond_norm_w': (1.0, 0.2)}
    factors = {}
    for name, (base, spread) in spreads.items():
        noise = np.random.default_rng([zlib.crc32(name.encode()), seed]).standard_normal(out[name].shape)
        drawn = base * np.exp(spread * noise) if base else spread * noise
        out[name] = jnp.asarray(drawn.astype(out[name].dtype))
    for name, factor in factors.items():
        out[name] = (out[name] * factor).astype(out[name].dtype)
    return out
```

```python
import concourse.bass as bass
from concourse import mybir
from contextlib import ExitStack

P = 128
B, L, DM = 2, 1024, 256
DI, DS = 512, 64
HEADS, HD = 16, 16
HP = 32
MH0, MH1 = 512, 1024
C = DM // P
NI = DI // P
HALF = 512
HALVES = L // HALF
CHUNKS = B * HALVES
HG = HEADS // 4
QT = L // P
BIG = 1.0e30
SUPER = NI * HALF
SCAN_TILES = 2 * B * HALVES * DS


def build(nc, t):
    F32, I32 = mybir.dt.float32, mybir.dt.int32
    ALU, ACT, AX = mybir.AluOpType, mybir.ActivationFunctionType, mybir.AxisListType

    ctx = ExitStack()
    with ctx:
        def sb(name, shape, dt=F32):
            return ctx.enter_context(nc.sbuf_tensor(name, shape, dt))

        def sem(name):
            return ctx.enter_context(nc.semaphore(name))

        arena = sb("arena", [P, 46592])

        def cut(at, *dims):
            n = 1
            for d in dims:
                n *= d
            v = arena[:, at:at + n]
            if len(dims) == 2:
                v = v.rearrange("p (a b) -> p a b", b=dims[1])
            if len(dims) == 3:
                v = v.rearrange("p (a b c) -> p a b c", b=dims[1], c=dims[2])
            if len(dims) == 4:
                v = v.rearrange("p (a b c d) -> p a b c d", b=dims[1], c=dims[2], d=dims[3])
            return v

        R_X, R_H, R_W = 0, 4096, 8192
        R_XS, R_DT, R_DTX, R_ZS = 13824, 17920, 22016, 26112
        R_DA, R_UH, R_BC = 30208, 34304, 42496

        x = cut(R_X, C, B, L)
        h = cut(R_H, C, B, L)
        in_w = cut(R_W, C, 2 * DI)
        xproj_w = cut(R_W + 2048, NI, DI + 2 * DS)
        out_w = cut(R_W + 4608, NI, DM)
        xs = cut(R_XS, NI, L)
        dt_ = cut(R_DT, NI, L)
        dtx = cut(R_DTX, NI, L)
        zs = cut(R_ZS, NI, L)
        decay = cut(R_DA, 2, NI, HALF)
        uh = cut(R_UH, 4, NI, HALF)
        bc = cut(R_BC, 2, 2, 2, HALF)

        mod_w = cut(R_UH, 2, C, 3 * DM)
        cond_w = cut(R_UH + 3072, 2, C, DM)
        w_up0 = cut(R_W, 2, C, MH0)
        w_down0 = cut(R_W + 2048, MH0 // P, DM)
        g0 = cut(R_DT, 2, MH0 // P, HALF)
        qkv_w = cut(R_DA, 3, C, HG, P)
        proj_w = cut(R_DA + 3072, HG, DM)
        w_up1 = cut(R_UH, C, 2 * MH1)
        w_down1 = cut(R_UH + 4096, MH1 // P, DM)
        qT = cut(R_XS, HG, L)
        kT = cut(R_DT, HG, L)
        v_aug = cut(R_DTX, QT, HG, P)
        attnT = cut(R_ZS, HG, L)
        probs = cut(R_BC, 3, 2, HALF)
        neg_max = cut(R_BC + 3072, QT, P)
        g1 = cut(R_XS, 2, MH1 // P, HALF)
        sq = cut(R_DTX, 2, C, HALF)
        rstd = cut(R_DTX + 2048, 2, HALF)

        mask_i = cut(R_XS, B, L)[0:1].bitcast(I32)
        mask_f = cut(R_XS + 2048, B, L)[0:1]
        mask_b = cut(R_UH + 6144, B, L)[0:1]

        bc_rows = sb("bc_rows", [P, L])
        attn_sb = sb("attn_sb", [P, 2, HALF])
        a_neg = sb("a_neg", [P, NI, DS])
        carry = sb("carry", [P, DS, NI])
        ident = sb("ident", [P, P])
        ones = sb("ones", [P, P])
        mean_w = sb("mean_w", [P, P])
        sum_sel = sb("sum_sel", [P, P])
        row16 = sb("row16", [1, 4, HP])
        row17 = sb("row17", [1, 4, HP])
        ones_row = sb("ones_row", [1, HALF])
        any_row = sb("any_row", [1, B])
        q_scale = sb("q_scale", [P, B])
        cond = sb("cond", [P, C, B])
        cond_silu = sb("cond_silu", [P, C, B])
        mod_b = sb("mod_b", [P, 2, 6])
        mods = sb("mods", [P, 2, 6, B])
        cond_b = sb("cond_b", [P, 2, C])
        cmod = sb("cmod", [P, 2, C, B])
        norm_w = sb("norm_w", [P, C])
        dt_bias = sb("dt_bias", [P, NI])
        d_skip = sb("d_skip", [P, NI])
        b_up1 = sb("b_up1", [P, 2 * MH1 // P])
        b_down1 = sb("b_down1", [P, C])
        b_proj = sb("b_proj", [P, C])
        eps = sb("eps", [P, 1])
        row_max = sb("row_max", [P, QT, HALVES, 4])
        top = sb("top", [P, QT, 4])

        psum = ctx.enter_context(nc.psum_tensor("psum", [P, 8, HALF], F32))
        bc_dram = nc.dram_tensor("bc_dram", [2 * B, P, L], F32).ap()

        names = """const_ready cond_in modw_in mask_in x_in norm_in ssm_w_in out_w_in ssm_small_in
            mlp0_in attn_w_in mlp1_in bc_out store_out
            cond_silu_ready mods_ready mods_step mask_step mask_ready any_full q_scale_ready
            tile_full tile_free_act tile_free_dve
            centred squared std_ready rstd_ready normed h_ready
            z_ready exp_step dt_raw softplus_ready dt_ready dtx_ready skip_ready bc_rows_ready a_exp a_ready
            decay_ready scan_done u_ready prod_done reduce_done carry_saved gated
            x_updated mid_step g_silu g_ready down_done
            pad_zero scores_full scores_free max_step top_ready neg_max_ready maxT_full q_final
            s2_full probs_ready pv_done attn_copied sums_full recip_ready attn_ready v_ready
            b_in_0 b_in_1 c_in_0 c_in_1 done_compute""".split()
        s = {n: sem(n) for n in names}

        eaters, first = [], {}

        def tiles(name, who):
            first[name] = len(eaters)
            eaters.extend(who)

        tiles("mods", "ddd")
        for name in ("ln0", "ln1", "rms0", "rms1"):
            if name == "ln1":
                for bd in range(2 * B):
                    tiles(f"xs{bd}", "a" * 16)
                    tiles(f"dt{bd}", "a" * 8)
                    tiles(f"bc{bd}", "d" * 2)
                    tiles(f"out{bd}.0", "d" * C)
                    tiles(f"out{bd}.1", "d" * C)
            if name == "rms1":
                for b in range(B):
                    tiles(f"qkv{b}", "a" * (2 * HG * HALVES + QT))
                    tiles(f"proj{b}", "d" * C * HALVES)
            tiles(name, ("d" * CHUNKS if name.startswith("ln") else "") + "a" * CHUNKS)
            if name in ("ln1", "rms1"):
                n_hidden = (MH0 if name == "ln1" else MH1) // P
                order = []
                for q in range(CHUNKS + 1):
                    if q < CHUNKS:
                        tiles(f"up{name}.{q}", "ad" * n_hidden)
                    if q:
                        tiles(f"down{name}.{q - 1}", "d" * C)

        def eaten(g, who):
            return sum(e == who for e in eaters[:g + 1])

        def bank(g):
            return psum[:, 4 + g % 4, :]

        def take(pe, g):
            if g >= 4:
                who = eaters[g - 4]
                pe.wait_ge(s["tile_free_act" if who == "a" else "tile_free_dve"], eaten(g - 4, who))
            return bank(g)

        BDS = [(d, b) for d in range(2) for b in range(B)]

        def half_order(d):
            return (0, 1) if d == 0 else (1, 0)

        def tok(half):
            return slice(half * HALF, (half + 1) * HALF)

        UPDATES = {}
        UPDATES["ssm"] = 2 * B * HALVES * C
        UPDATES["mlp0"] = UPDATES["ssm"] + CHUNKS * C
        UPDATES["attn"] = UPDATES["mlp0"] + CHUNKS * C
        UPDATES["mlp1"] = UPDATES["attn"] + CHUNKS * C
        NORMS = ("ln0", "ln1", "rms0", "rms1")
        BEFORE = {"ln0": 0, "ln1": UPDATES["ssm"], "rms0": UPDATES["mlp0"], "rms1": UPDATES["attn"]}

        block = ctx.enter_context(nc.Block())

        @block.sync
        def _(sp):
            def load(dst, src, name):
                sp.dma_start(dst, src).then_inc(s[name], 16)

            def kp(ap, n):
                return ap.rearrange("(c p) n -> p c n", p=P)

            load(cond[:, :, :], kp(t["cond"], B), "cond_in")
            for c in range(C):
                load(x[:, c, :, :], t["x"][:, c * P:(c + 1) * P, :].rearrange("b p t -> p b t"), "x_in")
            load(mod_w[:, 0], kp(t["mamba_w"], 0), "modw_in")
            load(mod_w[:, 1], kp(t["mlp_w"], 0), "modw_in")
            load(cond_w[:, 0], kp(t["shift_w"], 0), "modw_in")
            load(cond_w[:, 1], kp(t["scale_w"], 0), "modw_in")
            for k, name in enumerate(("mamba_b", "mlp_b")):
                load(mod_b[:, k, :], t[name], "modw_in")
            for k, name in enumerate(("shift_b", "scale_b")):
                load(cond_b[:, k, :], t[name], "modw_in")
            load(norm_w[:, :], t["norm_w"], "modw_in")
            load(b_up1[:, :], t["up1_b"], "norm_in")
            load(b_down1[:, :], t["down1_b"], "norm_in")
            load(b_proj[:, :], t["proj_b"], "norm_in")

            for n, (d, b) in enumerate(BDS):
                pre = ("fwd_", "bwd_")[d]
                if b == 0:
                    if n:
                        sp.wait_ge(s["tile_full"], first[f"bc{n - 1}"] + 2)
                        sp.wait_ge(s["decay_ready"], n * HALVES * DS)
                        sp.wait_ge(s["skip_ready"], n * NI)
                        sp.wait_ge(s["tile_full"], first[f"out{n - 1}.1"] + C)
                    load(in_w, kp(t[pre + "in_w"], 0), "ssm_w_in")
                    load(xproj_w, kp(t[pre + "xproj_w"], 0), "ssm_w_in")
                    load(out_w, kp(t[pre + "out_w"], 0), "ssm_w_in")
                    load(a_neg[:, :, :], kp(t[pre + "A_log"], 0), "ssm_small_in")
                    load(dt_bias[:, :], t[pre + "dt_bias"], "ssm_small_in")
                    load(d_skip[:, :], t[pre + "D"], "ssm_small_in")
                sp.wait_ge(s["bc_rows_ready"], 2 * (n + 1))
                sp.dma_start(bc_dram[n], bc_rows[:, :]).then_inc(s["bc_out"], 16)
                sp.wait_ge(s["bc_out"], 16 * (n + 1))
                for hi, half in enumerate(half_order(d)):
                    base = (n * HALVES + hi) * DS

                    def row_pair(pair, k, row):
                        if row == 0:
                            sp.wait_ge(s["u_ready"], pair * 2 + (base + 2))
                        else:
                            sp.wait_ge(s["prod_done"], pair * 2 + (base + 2))
                        src = bc_dram[n, bass.ds(pair * 2 + row * DS, 2), tok(half)]
                        sp.dma_start(bc[:, k, row], src.partition_broadcast(P))\
                          .then_inc(s[f"{'bc'[row]}_in_{k}"], 16)

                    row_pair(0, 0, 0)
                    with sp.Fori(0, DS // 4 - 1) as i:
                        for k in range(2):
                            row_pair(i * 2 + (k + 1), 1 - k, 0)
                            row_pair(i * 2 + k, k, 1)
                    row_pair(DS // 2 - 1, 1, 0)
                    row_pair(DS // 2 - 2, 0, 1)
                    row_pair(DS // 2 - 1, 1, 1)
            for k, name in enumerate(("mlp_w1", "mlp_w2")):
                load(w_up0[:, k], kp(t[name], 0), "mlp0_in")
            load(w_down0, kp(t["mlp_w3"], 0), "mlp0_in")
            sp.wait_ge(s["pad_zero"], 1)
            load(mask_i[:, :, :], t["mask"].rearrange("(a b) n -> a b n", a=1), "mask_in")
            for k in range(3):
                for c in range(C):
                    src = t["qkv_w"][c * P:(c + 1) * P, k * DM:(k + 1) * DM]
                    dst = qkv_w[:, k, c].rearrange("p g (j e) -> p (g j) e", e=HP)[:, :, 0:HD]
                    load(dst, src.rearrange("p (h e) -> p h e", e=HD), "attn_w_in")
            pr = t["proj_w"].rearrange("(g j e) n -> j e g n", j=4, e=HD)
            for j in range(4):
                load(proj_w[32 * j:32 * j + HD], pr[j], "attn_w_in")
            load(w_up1, kp(t["up1_w"], 0), "mlp1_in")
            load(w_down1, kp(t["down1_w"], 0), "mlp1_in")
            for q in range(CHUNKS):
                b, half = divmod(q, HALVES)
                sp.wait_ge(s["x_updated"], UPDATES["attn"] + C * (q + 1))
                for c in range(C):
                    sp.dma_start(t["out"][b, c * P:(c + 1) * P, tok(half)], x[:, c, b, tok(half)])\
                      .then_inc(s["store_out"], 16)
            sp.wait_ge(s["store_out"], 16 * CHUNKS * C)

        @block.gpsimd
        def _(pool):
            pool.memset(ident[:, :], 0.0).then_inc(s["const_ready"], 1)
            pool.memset(sum_sel[:, :], 0.0).then_inc(s["const_ready"], 1)
            pool.memset(ones[:, :], 1.0).then_inc(s["const_ready"], 1)
            pool.memset(mean_w[:, :], 1.0 / DM).then_inc(s["const_ready"], 1)
            pool.memset(row16[:, :, :], 0.0).then_inc(s["const_ready"], 1)
            pool.memset(row17[:, :, :], 0.0).then_inc(s["const_ready"], 1)
            pool.memset(ones_row[:, :], 1.0).then_inc(s["const_ready"], 1)
            pool.memset(eps[:, :], 1e-5).then_inc(s["const_ready"], 1)
            pool.wait_ge(s["const_ready"], 8)
            pool.affine_select(out=ident[:, :], in_=ident[:, :], compare_op=ALU.not_equal, fill=1.0,
                               base=0, pattern=[[-1, P]], channel_multiplier=1).then_inc(s["const_ready"], 1)
            sel = sum_sel[:, :].rearrange("p (j e) -> p j e", e=HP)
            pool.affine_select(out=sel, in_=sel, compare_op=ALU.not_equal, fill=1.0, base=-HD,
                               pattern=[[-HP, 4], [0, HP]], channel_multiplier=1).then_inc(s["const_ready"], 1)
            pool.memset(row16[:, :, HD:HD + 1], 1.0).then_inc(s["const_ready"], 1)
            pool.memset(row17[:, :, HD + 1:HD + 2], 1.0).then_inc(s["const_ready"], 1)

            for n, (d, b) in enumerate(BDS):
                pool.wait_ge(s["dt_ready"], n + 1)
                if n:
                    pass
                pool.tensor_tensor(dtx, dt_, xs, ALU.mult).then_inc(s["dtx_ready"], 1)
                pool.wait_ge(s["dtx_ready"], n + 1)
                for hi, half in enumerate(half_order(d)):
                    base = (n * HALVES + hi) * DS
                    with pool.Fori(0, DS // 4) as i:
                        for k in range(4):
                            if k % 2 == 0:
                                pool.wait_ge(s[f"b_in_{k // 2}"], i * 16 + (base // 4 + 1) * 16)
                            pool.wait_ge(s["reduce_done"], i * 4 + (base + k + 1))
                            b_row = bc[:, k // 2, 0, k % 2].unsqueeze(1).to_broadcast([P, NI, HALF])
                            pool.tensor_tensor(uh[:, k], dtx[:, :, tok(half)], b_row, ALU.mult)\
                                .then_inc(s["u_ready"], 1)
            pool.wait_ge(s["reduce_done"], SCAN_TILES + 4)
            pool.memset(arena[:, R_DA:R_DA + 4096], 0.0).then_inc(s["pad_zero"], 1)
            pool.memset(neg_max, 0.0).then_inc(s["pad_zero"], 1)

        @block.scalar
        def _(act):
            def norm(name):
                k = NORMS.index(name)
                off = CHUNKS * k
                centred = name.startswith("ln")
                tile0 = first[name] + (CHUNKS if centred else 0)
                for q in range(CHUNKS):
                    b, half = divmod(q, HALVES)
                    src = (h if centred else x)[:, :, b, tok(half)]
                    if centred:
                        act.wait_ge(s["centred"], (CHUNKS * k + q + 1) * C)
                    else:
                        act.wait_ge(s["x_updated"], BEFORE[name])
                    if q >= 2:
                        act.wait_ge(s["tile_full"], tile0 + q - 1)
                    act.activation(sq[:, q % 2], src, ACT.Square).then_inc(s["squared"], 1)
                    if q >= 1:
                        std(name, k, q - 1, tile0)
                std(name, k, CHUNKS - 1, tile0)

            def std(name, k, q, tile0):
                act.wait_ge(s["tile_full"], tile0 + q + 1)
                if q >= 2:
                    act.wait_ge(s["normed"], CHUNKS * k + q - 1)
                act.activation(rstd[:, q % 2], bank(tile0 + q), ACT.Sqrt,
                               bias=(eps[:, 0:1] if name.startswith("ln") else 0.0))\
                   .then_inc(s["tile_free_act"], 1)

            act.wait_ge(s["cond_in"], 16)
            act.activation(cond_silu[:, :, :], cond[:, :, :], ACT.Silu).then_inc(s["cond_silu_ready"], 1)
            act.wait_ge(s["const_ready"], 12)
            act.wait_ge(s["x_in"], 32)
            norm("ln0")

            for n, (d, b) in enumerate(BDS):
                if b == 0:
                    act.wait_ge(s["ssm_small_in"], 48 * (d + 1))
                    act.activation(a_neg[:, :, :], a_neg[:, :, :], ACT.Exp).then_inc(s["a_exp"], 1)
                if n:
                    act.wait_ge(s["reduce_done"], (n * HALVES) * DS + 4)
                    act.wait_ge(s["tile_full"], first[f"out{n - 1}.1"] + C)
                for m in range(16):
                    g = first[f"xs{n}"] + m
                    dst = (xs, zs)[m // 8][:, m % 8 // HALVES, tok(m % HALVES)]
                    act.wait_ge(s["tile_full"], g + 1)
                    act.activation(dst, bank(g), ACT.Silu).then_inc(s["tile_free_act"], 1)
                for m in range(8):
                    g = first[f"dt{n}"] + m
                    f, half = divmod(m, HALVES)
                    act.wait_ge(s["tile_full"], g + 1)
                    act.activation(dt_[:, f, tok(half)], bank(g), ACT.Identity, bias=dt_bias[:, f:f + 1])\
                       .then_inc(s["tile_free_act"], 1)
                act.wait_ge(s["tile_free_act"], eaten(first[f"dt{n}"] + 7, "a"))
                act.activation(dtx, dt_, ACT.Abs).then_inc(s["exp_step"], 1)
                act.wait_ge(s["exp_step"], 3 * n + 1)
                act.activation(dtx, dtx, ACT.Exp, scale=-1.0).then_inc(s["exp_step"], 1)
                act.wait_ge(s["exp_step"], 3 * n + 2)
                act.activation(dtx, dtx, ACT.Ln, bias=1.0).then_inc(s["exp_step"], 1)
                act.wait_ge(s["dtx_ready"], n + 1)
                for f in range(NI):
                    act.activation(xs[:, f], xs[:, f], ACT.Copy, scale=d_skip[:, f:f + 1])\
                       .then_inc(s["skip_ready"], 1)
                act.wait_ge(s["a_ready"], d + 1)
                for hi, half in enumerate(half_order(d)):
                    base = (n * HALVES + hi) * DS

                    def save(st, k):
                        act.wait_ge(s["scan_done"], st + (base + 3))
                        at = 0 if d == 1 else HALF - 1
                        act.activation(carry[:, bass.ds(st, 1), :].rearrange("p a b -> p (a b)"),
                                       uh[:, k, :, at], ACT.Copy).then_inc(s["carry_saved"], 1)

                    def decays(st, k, saves):
                        act.wait_ge(s["scan_done"], st + (base + 1))
                        if saves:
                            save(st - 2, (k + 2) % 4)
                        for f in range(NI):
                            e = act.activation(decay[:, k % 2, f], dt_[:, f, tok(half)], ACT.Exp,
                                               scale=a_neg[:, f, bass.ds(st, 1)])
                        e.then_inc(s["decay_ready"], 1)

                    for k in range(4):
                        decays(k, k, hi == 0 and k >= 2)
                    with act.Fori(1, DS // 4) as i:
                        for k in range(4):
                            decays(i * 4 + k, k, hi == 0)
                    if hi == 0:
                        save(DS - 2, 2)
                        save(DS - 1, 3)

            def mlp(name, n_hidden, gbuf, bias):
                chunk0 = 0 if name == "ln1" else CHUNKS
                silu0 = 0 if name == "ln1" else CHUNKS * MH0 // P
                for q in range(CHUNKS):
                    if q >= 2:
                        act.wait_ge(s["tile_full"], first[f"down{name}.{q - 2}"] + C)
                    for m in range(n_hidden):
                        g = first[f"up{name}.{q}"] + 2 * m
                        act.wait_ge(s["tile_full"], g + 1)
                        act.activation(gbuf[:, q % 2, m], bank(g), ACT.Silu,
                                       bias=(bias[:, m:m + 1] if bias is not None else 0.0))\
                           .then_inc(s["tile_free_act"], 1)

            norm("ln1")
            mlp("ln1", MH0 // P, g0, None)
            norm("rms0")
            act.wait_ge(s["any_full"], 1)
            act.activation(q_scale[:, :], psum[:, 0, 0:B], ACT.Copy, scale=HD ** -0.5)\
               .then_inc(s["q_scale_ready"], 1)
            act.wait_ge(s["q_scale_ready"], 1)
            for b in range(B):
                for m in range(2 * HG * HALVES):
                    g = first[f"qkv{b}"] + m
                    which, r = divmod(m, HG * HALVES)
                    hg, half = divmod(r, HALVES)
                    act.wait_ge(s["tile_full"], g + 1)
                    if m == 0:
                        act.wait_ge(s["h_ready"], 3 * CHUNKS * C)
                        if b:
                            act.wait_ge(s["attn_ready"], HG * HALVES * b)
                    if which == 0:
                        act.activation(qT[:, hg, tok(half)], bank(g), ACT.Copy, scale=q_scale[:, b:b + 1])\
                           .then_inc(s["tile_free_act"], 1)
                    else:
                        act.activation(kT[:, hg, tok(half)], bank(g), ACT.Copy).then_inc(s["tile_free_act"], 1)
                for kt in range(QT):
                    g = first[f"qkv{b}"] + 2 * HG * HALVES + kt
                    act.wait_ge(s["tile_full"], g + 1)
                    act.activation(v_aug[:, kt].rearrange("p g e -> p (g e)"), bank(g), ACT.Copy)\
                       .then_inc(s["tile_free_act"], 1)
                for hg in range(HG):
                    for qh in range(HALVES):
                        u = (b * HG + hg) * HALVES + qh
                        for m in range(2 * QT):
                            w = u * 2 * QT + m
                            act.wait_ge(s["s2_full"], w + 1)
                            if w >= 3:
                                act.wait_ge(s["pv_done"], w - 2)
                            sl = 2 * (w % 3)
                            act.activation(probs[:, w % 3], psum[:, sl:sl + 2, :], ACT.Exp)\
                               .then_inc(s["probs_ready"], 1)
                        act.wait_ge(s["pv_done"], (u + 1) * 2 * QT)
                        if u:
                            act.wait_ge(s["attn_ready"], u)
                        act.activation(attn_sb[:, 0], psum[:, 6], ACT.Copy).then_inc(s["attn_copied"], 1)
            norm("rms1")
            mlp("rms1", MH1 // P, g1, b_up1)

        @block.vector
        def _(dve):
            dve.memset(carry[:, :, :], 0.0).then_inc(s["reduce_done"], 4)
            dve.memset(top[:, :, :], 0.0).then_inc(s["scan_done"], 2)
            dve.memset(row_max[:, :, :, :], 0.0).then_inc(s["prod_done"], 4)
            dve.memset(attn_sb[:, :, :], 0.0).then_inc(s["u_ready"], 4)

            dve.wait_ge(s["modw_in"], 16 * 9)
            for k in range(2):
                g = first["mods"] + k
                dve.wait_ge(s["tile_full"], g + 1)
                dve.tensor_tensor(mods[:, k], bank(g)[:, 0:6 * B].rearrange("p (a b) -> p a b", b=B),
                                  mod_b[:, k, :].unsqueeze(2).to_broadcast([P, 6, B]), ALU.add)\
                   .then_inc(s["tile_free_dve"], 1)
            dve.wait_ge(s["tile_free_dve"], 2)
            dve.tensor_scalar(mods[:, :, C:2 * C, :], mods[:, :, C:2 * C, :], 1.0, None, ALU.add)\
               .then_inc(s["mods_ready"], 1)
            g = first["mods"] + 2
            dve.wait_ge(s["tile_full"], g + 1)
            dve.tensor_tensor(cmod[:, :, :, :], bank(g)[:, 0:2 * C * B].rearrange("p (k c b) -> p k c b", k=2, b=B),
                              cond_b[:, :, :].unsqueeze(3).to_broadcast([P, 2, C, B]), ALU.add)\
               .then_inc(s["tile_free_dve"], 1)
            dve.wait_ge(s["tile_free_dve"], 3)
            dve.tensor_scalar(cmod[:, 1], cmod[:, 1], 1.0, 0.1, ALU.add, ALU.max).then_inc(s["mods_step"], 1)
            dve.wait_ge(s["mods_step"], 1)
            dve.scalar_tensor_tensor(cmod[:, 1], cmod[:, 1], 10.0,
                                     norm_w[:, :].unsqueeze(2).to_broadcast([P, C, B]), ALU.min, ALU.mult)\
               .then_inc(s["mods_ready"], 1)
            dve.wait_ge(s["mods_ready"], 2)

            def norm(name):
                k = NORMS.index(name)
                centred = name.startswith("ln")
                tile0 = first[name] + (CHUNKS if centred else 0)
                if BEFORE[name]:
                    dve.wait_ge(s["x_updated"], BEFORE[name])
                if centred:
                    for q in range(CHUNKS):
                        b, half = divmod(q, HALVES)
                        g = first[name] + q
                        dve.wait_ge(s["tile_full"], g + 1)
                        for c in range(C):
                            o = dve.tensor_tensor(h[:, c, b, tok(half)], x[:, c, b, tok(half)], bank(g),
                                                  ALU.subtract).then_inc(s["centred"], 1)
                        dve.wait_ge(s["centred"], (CHUNKS * k + q + 1) * C)
                        dve.tensor_copy(top[:, 0, 0:1], top[:, 0, 1:2]).then_inc(s["tile_free_dve"], 1)
                for q in range(CHUNKS):
                    b, half = divmod(q, HALVES)
                    Q = CHUNKS * k + q
                    r = rstd[:, q % 2]
                    dve.wait_ge(s["tile_free_act"], eaten(tile0 + q, "a"))
                    if not centred:
                        dve.tensor_scalar(r, r, 1e-6, None, ALU.max).then_inc(s["mid_step"], 1)
                        dve.wait_ge(s["mid_step"], CHUNKS * (k - 2) + q + 1)
                    dve.reciprocal(r, r).then_inc(s["rstd_ready"], 1)
                    dve.wait_ge(s["rstd_ready"], Q + 1)
                    hq = h[:, :, b, tok(half)]
                    src = hq if centred else x[:, :, b, tok(half)]
                    dve.tensor_tensor(hq, src, r.unsqueeze(1).to_broadcast([P, C, HALF]), ALU.mult)\
                       .then_inc(s["normed"], 1)
                    dve.wait_ge(s["normed"], Q + 1)
                    for c in range(C):
                        if centred:
                            mul, add = mods[:, k, C + c, b:b + 1], mods[:, k, c, b:b + 1]
                        else:
                            mul, add = cmod[:, 1, c, b:b + 1], cmod[:, 0, c, b:b + 1]
                        dve.tensor_scalar(h[:, c, b, tok(half)], h[:, c, b, tok(half)], mul, add,
                                          ALU.mult, ALU.add).then_inc(s["h_ready"], 1)

            norm("ln0")

            for n, (d, b) in enumerate(BDS):
                for m in range(HALVES):
                    g = first[f"bc{n}"] + m
                    dve.wait_ge(s["tile_full"], g + 1)
                    if n and m == 0:
                        dve.wait_ge(s["bc_out"], 16 * n)
                    dve.tensor_copy(bc_rows[:, tok(m)], bank(g)).then_inc(s["tile_free_dve"], 1)
                dve.wait_ge(s["tile_free_dve"], eaten(first[f"bc{n}"] + 1, "d"))
                dve.tensor_copy(top[:, 0, 0:1], top[:, 0, 1:2]).then_inc(s["bc_rows_ready"], 2)
                if b == 0:
                    dve.wait_ge(s["a_exp"], d + 1)
                    dve.tensor_scalar(a_neg[:, :, :], a_neg[:, :, :], -1.0, None, ALU.mult).then_inc(s["a_ready"], 1)
                dve.wait_ge(s["exp_step"], 3 * n + 3)
                dve.scalar_tensor_tensor(dt_, dt_, 0.0, dtx, ALU.max, ALU.add).then_inc(s["dt_ready"], 1)

                rev = d == 1

                def along(ap):
                    return ap[:, ::-1] if rev else ap

                for hi, half in enumerate(half_order(d)):
                    base = (n * HALVES + hi) * DS

                    def scan(st, k):
                        dve.wait_ge(s["decay_ready"], st + (base + 1))
                        dve.wait_ge(s["u_ready"], st + (base + 5))
                        for f in range(NI):
                            start = carry[:, bass.ds(st, 1), f] if hi else 0.0
                            o = dve.tensor_tensor_scan(along(uh[:, k, f]), along(decay[:, k % 2, f]),
                                                       along(uh[:, k, f]), start, op0=ALU.mult, op1=ALU.add)
                        o.then_inc(s["scan_done"], 1)

                    def weigh(st, k):
                        dve.wait_ge(s["scan_done"], st + (base + 3))
                        if hi == 0:
                            dve.wait_ge(s["carry_saved"], st + (DS * n + 1))
                        if k % 2 == 0:
                            dve.wait_ge(s[f"c_in_{k // 2}"], (base // 4 + 1) * 16 + (st - k) * 4)
                        c_row = bc[:, k // 2, 1, k % 2].unsqueeze(1).to_broadcast([P, NI, HALF])
                        dve.tensor_tensor(uh[:, k], uh[:, k], c_row, ALU.mult).then_inc(s["prod_done"], 1)

                    if hi:
                        dve.wait_ge(s["carry_saved"], DS * (n + 1))
                    scan(0, 0)
                    with dve.Fori(0, DS // 4 - 1) as i:
                        for k in range(4):
                            scan(i * 4 + (k + 1), (k + 1) % 4)
                            weigh(i * 4 + k, k)
                    for k in range(4):
                        if k < 3:
                            scan(DS - 4 + k + 1, k + 1)
                        weigh(DS - 4 + k, k)
                    dve.wait_ge(s["reduce_done"], base + DS + 4)
                    dve.tensor_tensor(zs[:, :, tok(half)], psum[:, 0:4, :], zs[:, :, tok(half)], ALU.mult)\
                       .then_inc(s["gated"], 1)
                    for c in range(C):
                        g = first[f"out{n}.{hi}"] + c
                        xc = x[:, c, b, tok(half)]
                        dve.wait_ge(s["tile_full"], g + 1)
                        dve.scalar_tensor_tensor(xc, bank(g), mods[:, 0, 2 * C + c, b:b + 1], xc, ALU.mult, ALU.add)\
                           .then_inc(s["x_updated"], 1)
                        dve.wait_ge(s["x_updated"], (n * HALVES + hi) * C + c + 1)
                        dve.tensor_copy(top[:, 0, 0:1], top[:, 0, 1:2]).then_inc(s["tile_free_dve"], 1)

            def mlp(name, n_hidden, gbuf, up_bias, finish, done0):
                for q in range(CHUNKS + 1):
                    if q < CHUNKS:
                        for m in range(n_hidden):
                            g = first[f"up{name}.{q}"] + 2 * m + 1
                            gm = gbuf[:, q % 2, m]
                            dve.wait_ge(s["tile_full"], g + 1)
                            dve.wait_ge(s["tile_free_act"], eaten(g - 1, "a"))
                            add = up_bias[:, n_hidden + m:n_hidden + m + 1] if up_bias is not None else 0.0
                            dve.scalar_tensor_tensor(gm, bank(g), add, gm, ALU.add, ALU.mult)\
                               .then_inc(s["tile_free_dve"], 1)
                    if q:
                        b, half = divmod(q - 1, HALVES)
                        for c in range(C):
                            g = first[f"down{name}.{q - 1}"] + c
                            xc = x[:, c, b, tok(half)]
                            dve.wait_ge(s["tile_full"], g + 1)
                            finish(xc, bank(g), c, b).then_inc(s["x_updated"], 1)
                            dve.wait_ge(s["x_updated"], done0 + (q - 1) * C + c + 1)
                            dve.tensor_copy(top[:, 0, 0:1], top[:, 0, 1:2]).then_inc(s["tile_free_dve"], 1)

            dve.wait_ge(s["mask_in"], 16)
            dve.tensor_scalar(mask_f[:, :, :], mask_i[:, :, :], 0.0, None, ALU.not_equal).then_inc(s["mask_step"], 1)
            dve.wait_ge(s["mask_step"], 1)
            dve.tensor_reduce(any_row[:, :], mask_f[:, :, :], axis=AX.X, op=ALU.max).then_inc(s["mask_step"], 1)
            dve.tensor_scalar(mask_b[:, :, :], mask_f[:, :, :], -1.0, BIG, ALU.add, ALU.mult)\
               .then_inc(s["mask_step"], 1)
            dve.wait_ge(s["mask_step"], 3)
            for b in range(B):
                dve.tensor_scalar(mask_b[:, b, :], mask_b[:, b, :], any_row[:, b:b + 1], None, ALU.mult)\
                   .then_inc(s["mask_ready"], 1)

            norm("ln1")
            mlp("ln1", MH0 // P, g0, None,
                lambda xc, y, c, b: dve.scalar_tensor_tensor(xc, y, mods[:, 1, 2 * C + c, b:b + 1], xc,
                                                             ALU.mult, ALU.add), UPDATES["ssm"])
            norm("rms0")
            for b in range(B):
                dve.wait_ge(s["tile_free_act"], eaten(first[f"qkv{b}"] + 2 * HG * HALVES + QT - 1, "a"))
                dve.memset(v_aug.rearrange("p t g (j e) -> p t (g j) e", e=HP)[:, :, :, HD:HD + 1], 1.0)\
                   .then_inc(s["v_ready"], 1)
                for hg in range(HG):
                    u = b * HG + hg
                    for m in range(QT * HALVES):
                        qt, kh = divmod(m, HALVES)
                        w = u * QT * HALVES + m
                        dve.wait_ge(s["scores_full"], w + 1)
                        if m == 0 and u:
                            dve.wait_ge(s["top_ready"], u)
                        dve.tensor_reduce(row_max[:, qt, kh, :], psum[:, 4 * kh:4 * kh + 4, :], axis=AX.X,
                                          op=ALU.max).then_inc(s["scores_free"], 1)
                    dve.wait_ge(s["scores_free"], (u + 1) * QT * HALVES)
                    if u == 0:
                        dve.wait_ge(s["pad_zero"], 2)
                    dve.tensor_tensor(top[:, :, :], row_max[:, :, 0, :], row_max[:, :, 1, :], ALU.max)\
                       .then_inc(s["top_ready"], 1)
                    dve.wait_ge(s["top_ready"], u + 1)
                    if u:
                        dve.wait_ge(s["maxT_full"], u)
                    dve.tensor_scalar(neg_max[:, :, HD:P:HP], top[:, :, :], -1.0, None, ALU.mult)\
                       .then_inc(s["neg_max_ready"], 1)
                    dve.wait_ge(s["maxT_full"], u + 1)
                    dve.tensor_tensor(qT[:, hg].rearrange("p (a t) -> p a t", a=HALVES),
                                      qT[:, hg].rearrange("p (a t) -> p a t", a=HALVES), psum[:, 0:2, :], ALU.add)\
                       .then_inc(s["q_final"], 1)
                    for qh in range(HALVES):
                        v = u * HALVES + qh
                        dve.wait_ge(s["sums_full"], v + 1)
                        dve.reciprocal(attn_sb[:, 1], psum[:, 7]).then_inc(s["recip_ready"], 1)
                        dve.wait_ge(s["recip_ready"], v + 1)
                        if b and hg == 0 and qh == 0:
                            dve.wait_ge(s["x_updated"], UPDATES["mlp0"] + C * HALVES)
                        dve.tensor_tensor(attnT[:, hg, tok(qh)], attn_sb[:, 0], attn_sb[:, 1], ALU.mult)\
                           .then_inc(s["attn_ready"], 1)
                for m in range(C * HALVES):
                    half, c = divmod(m, C)
                    g = first[f"proj{b}"] + m
                    xc = x[:, c, b, tok(half)]
                    dve.wait_ge(s["tile_full"], g + 1)
                    dve.scalar_tensor_tensor(xc, bank(g), b_proj[:, c:c + 1], xc, ALU.add, ALU.add)\
                       .then_inc(s["x_updated"], 1)
                    dve.wait_ge(s["x_updated"], UPDATES["mlp0"] + b * C * HALVES + m + 1)
                    dve.tensor_copy(top[:, 0, 0:1], top[:, 0, 1:2]).then_inc(s["tile_free_dve"], 1)
            norm("rms1")
            mlp("rms1", MH1 // P, g1, b_up1,
                lambda xc, y, c, b: dve.scalar_tensor_tensor(xc, y, b_down1[:, c:c + 1], xc, ALU.add, ALU.add),
                UPDATES["attn"])

        @block.tensor
        def _(pe):
            def product(dst, pairs, last=None):
                for k, (lhsT, rhs) in enumerate(pairs):
                    o = pe.matmul(dst, lhsT, rhs, start=k == 0, stop=k == len(pairs) - 1)
                return o

            def norm(name):
                k = NORMS.index(name)
                centred = name.startswith("ln")
                if BEFORE[name]:
                    pe.wait_ge(s["x_updated"], BEFORE[name])
                if centred:
                    for q in range(CHUNKS):
                        b, half = divmod(q, HALVES)
                        dst = take(pe, first[name] + q)
                        product(dst, [(mean_w[:, :], x[:, c, b, tok(half)]) for c in range(C)])\
                            .then_inc(s["tile_full"], 1)
                tile0 = first[name] + (CHUNKS if centred else 0)
                for q in range(CHUNKS):
                    pe.wait_ge(s["squared"], CHUNKS * k + q + 1)
                    dst = take(pe, tile0 + q)
                    product(dst, [(mean_w[:, :], sq[:, q % 2, c]) for c in range(C)]).then_inc(s["tile_full"], 1)

            pe.wait_ge(s["const_ready"], 12)
            pe.wait_ge(s["modw_in"], 16 * 9)
            for k in range(2):
                dst = take(pe, first["mods"] + k)
                for m in range(6):
                    o = product(dst[:, m * B:(m + 1) * B],
                                [(mod_w[:, k, c, m * P:(m + 1) * P], cond[:, c, :]) for c in range(C)])
                o.then_inc(s["tile_full"], 1)
            pe.wait_ge(s["cond_silu_ready"], 1)
            dst = take(pe, first["mods"] + 2)
            for k in range(2):
                for m in range(C):
                    r = (k * C + m) * B
                    o = product(dst[:, r:r + B],
                                [(cond_w[:, k, c, m * P:(m + 1) * P], cond_silu[:, c, :]) for c in range(C)])
            o.then_inc(s["tile_full"], 1)
            pe.wait_ge(s["x_in"], 32)
            norm("ln0")
            pe.wait_ge(s["h_ready"], CHUNKS * C)

            for n, (d, b) in enumerate(BDS):
                if b == 0:
                    pe.wait_ge(s["ssm_w_in"], 16 * 3 * (d + 1))
                for m in range(16):
                    path, r = divmod(m, 8)
                    f, half = divmod(r, HALVES)
                    dst = take(pe, first[f"xs{n}"] + m)
                    pairs = []
                    for c in range(C):
                        w = in_w[:, c, path * DI + f * P:path * DI + (f + 1) * P]
                        pairs.append((w, h[:, c, b, tok(half)]))
                    product(dst, pairs).then_inc(s["tile_full"], 1)
                pe.wait_ge(s["tile_free_act"], eaten(first[f"xs{n}"] + 7, "a"))
                for m in range(10):
                    f, half = divmod(m, HALVES)
                    dst = take(pe, first[f"dt{n}"] + m)
                    product(dst, [(xproj_w[:, c, f * P:(f + 1) * P], xs[:, c, tok(half)]) for c in range(NI)])\
                        .then_inc(s["tile_full"], 1)

                for hi, half in enumerate(half_order(d)):
                    base = (n * HALVES + hi) * DS

                    def reduce(rhs, start, stop):
                        for f in range(NI):
                            o = pe.matmul(psum[:, f, :], ident[:, :], rhs[:, f, :], start=start, stop=stop)
                        return o

                    pe.wait_ge(s["skip_ready"], NI * (n + 1))
                    if n or hi:
                        pe.wait_ge(s["gated"], n * HALVES + hi)
                    reduce(xs[:, :, tok(half)], True, False)
                    with pe.Fori(0, DS // 4 - 1) as i:
                        for k in range(4):
                            pe.wait_ge(s["prod_done"], i * 4 + (base + k + 5))
                            reduce(uh[:, k], False, False).then_inc(s["reduce_done"], 1)
                    for k in range(4):
                        pe.wait_ge(s["prod_done"], base + DS - 4 + k + 5)
                        reduce(uh[:, k], False, k == 3).then_inc(s["reduce_done"], 1)
                    pe.wait_ge(s["gated"], n * HALVES + hi + 1)
                    for c in range(C):
                        dst = take(pe, first[f"out{n}.{hi}"] + c)
                        product(dst, [(out_w[:, f, c * P:(c + 1) * P], zs[:, f, tok(half)]) for f in range(NI)])\
                            .then_inc(s["tile_full"], 1)

            def mlp(name, n_hidden, gbuf, weights, down):
                for q in range(CHUNKS + 1):
                    if q < CHUNKS:
                        b, half = divmod(q, HALVES)
                        for m in range(2 * n_hidden):
                            hidden, which = divmod(m, 2)
                            dst = take(pe, first[f"up{name}.{q}"] + m)
                            product(dst, [(weights(c, which, hidden), h[:, c, b, tok(half)]) for c in range(C)])\
                                .then_inc(s["tile_full"], 1)
                    if q:
                        pe.wait_ge(s["tile_free_dve"], eaten(first[f"up{name}.{q - 1}"] + 2 * n_hidden - 1, "d"))
                        for c in range(C):
                            dst = take(pe, first[f"down{name}.{q - 1}"] + c)
                            product(dst, [(down[:, m, c * P:(c + 1) * P], gbuf[:, (q - 1) % 2, m])
                                          for m in range(n_hidden)]).then_inc(s["tile_full"], 1)

            norm("ln1")
            pe.wait_ge(s["mlp0_in"], 48)
            pe.wait_ge(s["h_ready"], 2 * CHUNKS * C)
            mlp("ln1", MH0 // P, g0, lambda c, which, m: w_up0[:, which, c, m * P:(m + 1) * P], w_down0)
            norm("rms0")
            pe.wait_ge(s["attn_w_in"], 160)
            pe.wait_ge(s["h_ready"], 3 * CHUNKS * C)
            pe.wait_ge(s["mask_ready"], B)
            pe.matmul(psum[:, 0, 0:B], ones[0:1, :], any_row[:, :], start=True, stop=True).then_inc(s["any_full"], 1)
            for b in range(B):
                for m in range(2 * HG * HALVES):
                    which, r = divmod(m, HG * HALVES)
                    hg, half = divmod(r, HALVES)
                    dst = take(pe, first[f"qkv{b}"] + m)
                    pairs = [(qkv_w[:, which, c, hg], h[:, c, b, tok(half)]) for c in range(C)]
                    if which == 0:
                        pairs.append((row17[:, :, :].rearrange("p j e -> p (j e)"), ones_row[:, :]))
                    else:
                        pairs.append((row16[:, :, :].rearrange("p j e -> p (j e)"), ones_row[:, :]))
                        pairs.append((row17[:, :, :].rearrange("p j e -> p (j e)"), mask_b[:, b, tok(half)]))
                    product(dst, pairs).then_inc(s["tile_full"], 1)
                for kt in range(QT):
                    dst = take(pe, first[f"qkv{b}"] + 2 * HG * HALVES + kt)
                    product(dst, [(h[:, c, b, kt * P:(kt + 1) * P], qkv_w[:, 2, c].rearrange("p g e -> p (g e)"))
                                  for c in range(C)]).then_inc(s["tile_full"], 1)
                pe.wait_ge(s["tile_free_act"], eaten(first[f"qkv{b}"] + 2 * HG * HALVES + QT - 1, "a"))
                pe.wait_ge(s["q_scale_ready"], 1)
                pe.wait_ge(s["v_ready"], b + 1)
                for hg in range(HG):
                    u = b * HG + hg
                    if u:
                        pe.wait_ge(s["probs_ready"], u * HALVES * 2 * QT)
                        pe.wait_ge(s["attn_ready"], u * HALVES)
                    for m in range(QT * HALVES):
                        qt, kh = divmod(m, HALVES)
                        w = u * QT * HALVES + m
                        if m >= 2:
                            pe.wait_ge(s["scores_free"], w - 1)
                        for j in range(4):
                            o = pe.matmul(psum[:, 4 * kh + j, :], qT[32 * j:32 * j + 32, hg, qt * P:(qt + 1) * P],
                                          kT[32 * j:32 * j + 32, hg, tok(kh)], start=True, stop=True)
                        o.then_inc(s["scores_full"], 1)
                    pe.wait_ge(s["neg_max_ready"], u + 1)
                    for qt in range(QT):
                        o = pe.transpose(psum[:, qt // 4, qt % 4 * P:qt % 4 * P + P], neg_max[:, qt, :], ident[:, :])
                    o.then_inc(s["maxT_full"], 1)
                    pe.wait_ge(s["q_final"], u + 1)
                    for qh in range(HALVES):
                        v = u * HALVES + qh

                        def scores2(m):
                            kt, pair = divmod(m, 2)
                            w = v * 2 * QT + m
                            if w >= 3:
                                pe.wait_ge(s["probs_ready"], w - 2)
                            for jj in range(2):
                                j = 2 * pair + jj
                                o = pe.matmul(psum[:, 2 * (w % 3) + jj, :], kT[32 * j:32 * j + 32, hg, kt * P:(kt + 1) * P],
                                              qT[32 * j:32 * j + 32, hg, tok(qh)], start=True, stop=True)
                            o.then_inc(s["s2_full"], 1)

                        def weigh_v(m):
                            kt, pair = divmod(m, 2)
                            w = v * 2 * QT + m
                            pe.wait_ge(s["probs_ready"], w + 1)
                            if v and m == 0:
                                pe.wait_ge(s["attn_copied"], v)
                            for jj in range(2):
                                j = 2 * pair + jj
                                o = pe.matmul(psum[32 * j:32 * j + 32, 6, :], v_aug[:, kt, hg, 32 * j:32 * j + 32],
                                              probs[:, w % 3, jj], start=kt == 0, stop=kt == QT - 1)
                            o.then_inc(s["pv_done"], 1)

                        scores2(0)
                        scores2(1)
                        for m in range(2 * QT):
                            if m + 2 < 2 * QT:
                                scores2(m + 2)
                            weigh_v(m)
                        pe.wait_ge(s["attn_copied"], v + 1)
                        if v:
                            pe.wait_ge(s["recip_ready"], v)
                        pe.matmul(psum[:, 7, :], sum_sel[:, :], attn_sb[:, 0], start=True, stop=True)\
                          .then_inc(s["sums_full"], 1)
                pe.wait_ge(s["attn_ready"], (b + 1) * HG * HALVES)
                for m in range(C * HALVES):
                    half, c = divmod(m, C)
                    dst = take(pe, first[f"proj{b}"] + m)
                    product(dst, [(proj_w[:, hg, c * P:(c + 1) * P], attnT[:, hg, tok(half)]) for hg in range(HG)])\
                        .then_inc(s["tile_full"], 1)
            norm("rms1")
            pe.wait_ge(s["mlp1_in"], 32)
            pe.wait_ge(s["norm_in"], 48)
            pe.wait_ge(s["h_ready"], 4 * CHUNKS * C)
            mlp("rms1", MH1 // P, g1,
                lambda c, which, m: w_up1[:, c, which * MH1 + m * P:which * MH1 + (m + 1) * P], w_down1)


def kernel(**inputs):
    import numpy as np
    import concourse.bacc as bacc
    from concourse.bass_utils import run_bass_kernel_spmd

    g = {k: np.asarray(v) for k, v in inputs.items()}
    l0, l1 = "L0_cond_", "L1_cond_"

    def lay(a):
        return np.ascontiguousarray(a)

    arrays = {
        "x": lay(g["x"].transpose(0, 2, 1)),
        "cond": lay(g["cond_1024"].T),
        "mask": lay(g["mask_BxS_ik0"]),
        "mamba_w": lay(g[l0 + "adaln_mamba_w"]), "mamba_b": lay(g[l0 + "adaln_mamba_b"]),
        "mlp_w": lay(g[l0 + "adaln_mlp_w"]), "mlp_b": lay(g[l0 + "adaln_mlp_b"]),
        "mlp_w1": lay(g[l0 + "mlp_w1"]), "mlp_w2": lay(g[l0 + "mlp_w2"]), "mlp_w3": lay(g[l0 + "mlp_w3"]),
        "norm_w": lay(g[l1 + "norm_w"]),
        "scale_w": lay(g[l1 + "scale_w"].T), "scale_b": lay(g[l1 + "scale_b"]),
        "shift_w": lay(g[l1 + "shift_w"].T), "shift_b": lay(g[l1 + "shift_b"]),
        "qkv_w": lay(g[l1 + "qkv_w"].T),
        "proj_w": lay(g[l1 + "proj_w"].T), "proj_b": lay(g[l1 + "proj_b"]),
        "up1_w": lay(g[l1 + "mlp_w1"].T), "up1_b": lay(g[l1 + "mlp_b1"]),
        "down1_w": lay(g[l1 + "mlp_w2"].T), "down1_b": lay(g[l1 + "mlp_b2"]),
    }
    for pre in ("fwd_", "bwd_"):
        for name in ("in_w", "xproj_w", "dt_bias", "A_log", "D", "out_w"):
            arrays[pre + name] = lay(g[l0 + pre + name])
    arrays = {k: lay(a.reshape(-1, P).T) if a.ndim == 1 else a for k, a in arrays.items()}

    nc = bacc.Bacc("TRN2", target_bir_lowering=False, num_devices=1)
    t = {k: nc.dram_tensor(f"in_{k}", a.shape, mybir.dt.from_np(a.dtype), kind="ExternalInput").ap()
         for k, a in arrays.items()}
    t["out"] = nc.dram_tensor("out_xT", (B, DM, L), mybir.dt.float32, kind="ExternalOutput").ap()
    build(nc, t)
    r = run_bass_kernel_spmd(nc, [{f"in_{k}": a for k, a in arrays.items()}], core_ids=[0])
    return lay(r.results[0]["out_xT"].transpose(0, 2, 1))
```

```python
import concourse.bass as bass
from concourse import mybir
from contextlib import ExitStack

P = 128
B, L, DM = 2, 1024, 256
DI, DS = 512, 64
HEADS, HD = 16, 16
HP = 32
MH0, MH1 = 512, 1024
C = DM // P
NI = DI // P
HALF = 512
HALVES = L // HALF
CHUNKS = B * HALVES
HG = HEADS // 4
QT = L // P
BIG = 1.0e30
PARTS = 3
Q_PARTS = (0, 0, 1, 0, 2, 1)
K_PARTS = (0, 1, 0, 2, 0, 1)
PLAIN = 6 * HD + 1
ROWS = PLAIN + PARTS
ONE_ROW = 6 * HD
LOADS = 16 * (12 + 1)
TWO_ONES = 1.0 + 2.0 ** -9 - 2.0 ** -16
BLOCK = 2 * QT
SCAN_TILES = 2 * B * HALVES * DS


def build(nc, t):
    F32, I32, BF16 = mybir.dt.float32, mybir.dt.int32, mybir.dt.bfloat16
    ALU, ACT, AX = mybir.AluOpType, mybir.ActivationFunctionType, mybir.AxisListType

    ctx = ExitStack()
    with ctx:
        def sb(name, shape, dt=F32):
            return ctx.enter_context(nc.sbuf_tensor(name, shape, dt))

        def sem(name):
            return ctx.enter_context(nc.semaphore(name))

        arena = sb("arena", [P, 46592])

        def cut(at, *dims):
            n = 1
            for d in dims:
                n *= d
            v = arena[:, at:at + n]
            if len(dims) == 2:
                v = v.rearrange("p (a b) -> p a b", b=dims[1])
            if len(dims) == 3:
                v = v.rearrange("p (a b c) -> p a b c", b=dims[1], c=dims[2])
            if len(dims) == 4:
                v = v.rearrange("p (a b c d) -> p a b c d", b=dims[1], c=dims[2], d=dims[3])
            return v

        R_X, R_H, R_W = 0, 4096, 8192
        R_XS, R_DT, R_DTX, R_ZS = 13824, 17920, 22016, 26112
        R_DA, R_UH, R_BC = 30208, 34304, 42496

        x = cut(R_X, C, B, L)
        h = cut(R_H, C, B, L)
        in_w = cut(R_W, C, 2 * DI)
        xproj_w = cut(R_W + 2048, NI, DI + 2 * DS)
        out_w = cut(R_W + 4608, NI, DM)
        xs = cut(R_XS, NI, L)
        dt_ = cut(R_DT, NI, L)
        dtx = cut(R_DTX, NI, L)
        zs = cut(R_ZS, NI, L)
        decay = cut(R_DA, 2, NI, HALF)
        uh = cut(R_UH, 4, NI, HALF)
        bc = cut(R_BC, 2, 2, 2, HALF)

        mod_w = cut(R_UH, 2, C, 3 * DM)
        cond_w = cut(R_UH + 3072, 2, C, DM)
        w_up0 = cut(R_W, 2, C, MH0)
        w_down0 = cut(R_W + 2048, MH0 // P, DM)
        g0 = cut(R_DT, 2, MH0 // P, HALF)
        qk_w = cut(R_DA, 2, C, DM)
        v_w = cut(R_DA + 1024, C, HG, P)
        proj_w = cut(R_DA + 2048, HG, DM)
        w_up1 = cut(R_UH, C, 2 * MH1)
        w_down1 = cut(R_UH + 4096, MH1 // P, DM)
        qk = cut(R_BC, 2, C, L)
        qk_parts = cut(R_XS, 6144).bitcast(BF16).rearrange("p (a w c t) -> p a w c t", a=PARTS, w=2, c=C)
        stack = cut(R_XS, 8192).bitcast(BF16).rearrange("p (u w j t) -> p u w j t", u=2, w=2, j=4)
        v_aug = cut(R_DTX, B, QT, HG, P)
        attnT = [cut(R_H, HG, L), cut(R_DTX, HG, L)]
        probs = cut(R_BC, 3, 2, HALF)
        g1 = cut(R_XS, 2, MH1 // P, HALF)
        sq = cut(R_DTX, 2, C, HALF)
        rstd = cut(R_DTX + 2048, 2, HALF)

        mask_i = cut(R_XS, B, L)[0:1].bitcast(I32)
        mask_f = cut(R_XS + 2048, B, L)[0:1]
        mask_d = cut(R_XS, B, L)[0:1]
        mask_b = cut(R_UH + 6144, L)[0:1].bitcast(BF16).rearrange("p (b t) -> p b t", b=B)

        bc_rows = sb("bc_rows", [P, L])
        attn_sb = sb("attn_sb", [P, 2, HALF])
        a_neg = sb("a_neg", [P, NI, DS])
        carry = sb("carry", [P, DS, NI])
        ident = sb("ident", [P, P])
        ones = sb("ones", [P, P])
        mean_w = sb("mean_w", [P, P])
        ident_b = sb("ident_b", [P, P], BF16)
        sum_sel = sb("sum_sel", [P, P])
        any_row = sb("any_row", [1, B])
        q_scale = sb("q_scale", [P, B])
        cond = sb("cond", [P, C, B])
        cond_silu = sb("cond_silu", [P, C, B])
        mod_b = sb("mod_b", [P, 2, 6])
        mods = sb("mods", [P, 2, 6, B])
        cond_b = sb("cond_b", [P, 2, C])
        cmod = sb("cmod", [P, 2, C, B])
        norm_w = sb("norm_w", [P, C])
        dt_bias = sb("dt_bias", [P, NI])
        d_skip = sb("d_skip", [P, NI])
        b_up1 = sb("b_up1", [P, 2 * MH1 // P])
        b_down1 = sb("b_down1", [P, C])
        b_proj = sb("b_proj", [P, C])
        eps = sb("eps", [P, 1])
        row_max = sb("row_max", [P, QT, 4, HALVES])
        top = sb("top", [P, QT, 4])
        top_rest = sb("top_rest", [P, QT, 4])
        top_parts = sb("top_parts", [P, QT, 4, 4], BF16)

        psum = ctx.enter_context(nc.psum_tensor("psum", [P, 8, HALF], F32))
        qk_dram = nc.dram_tensor("qk_dram", [B, PARTS, 2, DM, L], BF16).ap()
        bc_dram = nc.dram_tensor("bc_dram", [2 * B, P, L], F32).ap()

        names = """const_ready cond_in modw_in mask_in x_in norm_in ssm_w_in out_w_in ssm_small_in
            mlp0_in attn_w_in mlp1_in bc_out store_out
            cond_silu_ready mods_ready mods_step mask_step mask_ready any_full q_scale_ready
            tile_full tile_free_act tile_free_dve
            centred squared std_ready rstd_ready normed h_ready
            z_ready exp_step dt_raw softplus_ready dt_ready dtx_ready skip_ready bc_rows_ready a_exp a_ready
            decay_ready scan_done u_ready prod_done reduce_done carry_saved gated
            x_updated mid_step g_silu g_ready down_done
            pad_zero scores_full scores_free max_step top_ready rows_full_0 rows_full_1 rows_ready_0 rows_ready_1
            hi_ready rest_ready mid_ready lo_ready qk_out ones_set stack_in_0 stack_in_1
            s2_full probs_ready pv_done attn_copied sums_full recip_ready attn_ready v_ready
            b_in_0 b_in_1 c_in_0 c_in_1 done_compute""".split()
        s = {n: sem(n) for n in names}

        FREES = {"a": ("tile_free_act", 1), "d": ("tile_free_dve", 1), "x": ("x_updated", 1),
                 "c": ("centred", C), "r": ("bc_rows_ready", 1)}
        eaters, first = [], {}

        def tiles(name, who):
            first[name] = len(eaters)
            eaters.extend(who)

        tiles("mods", "ddd")
        for name in ("ln0", "ln1", "rms0", "rms1"):
            if name == "ln1":
                for bd in range(2 * B):
                    tiles(f"xs{bd}", "a" * 16)
                    tiles(f"dt{bd}", "a" * 8)
                    tiles(f"bc{bd}", "r" * HALVES)
                    tiles(f"out{bd}.0", "x" * C)
                    tiles(f"out{bd}.1", "x" * C)
            if name == "rms1":
                for b in range(B):
                    tiles(f"qk{b}", "a" * (2 * C * HALVES))
                    tiles(f"v{b}", "a" * QT)
                tiles("proj", "x" * C * CHUNKS)
            tiles(name, ("c" * CHUNKS if name.startswith("ln") else "") + "a" * CHUNKS)
            if name in ("ln1", "rms1"):
                n_hidden = (MH0 if name == "ln1" else MH1) // P
                order = []
                for q in range(CHUNKS + 1):
                    if q < CHUNKS:
                        tiles(f"up{name}.{q}", "ad" * n_hidden)
                    if q:
                        tiles(f"down{name}.{q - 1}", "x" * C)

        def eaten(g, who):
            return sum(e == who for e in eaters[:g + 1])

        def bank(g):
            return psum[:, 4 + g % 4, :]

        def take(pe, g):
            if g >= 4:
                name, each = FREES[eaters[g - 4]]
                pe.wait_ge(s[name], each * eaten(g - 4, eaters[g - 4]))
            return bank(g)

        BDS = [(d, b) for d in range(2) for b in range(B)]

        def half_order(d):
            return (0, 1) if d == 0 else (1, 0)

        def tok(half):
            return slice(half * HALF, (half + 1) * HALF)

        UPDATES = {}
        UPDATES["ssm"] = 2 * B * HALVES * C
        UPDATES["mlp0"] = UPDATES["ssm"] + CHUNKS * C
        UPDATES["attn"] = UPDATES["mlp0"] + CHUNKS * C
        UPDATES["mlp1"] = UPDATES["attn"] + CHUNKS * C
        NORMS = ("ln0", "ln1", "rms0", "rms1")
        BEFORE = {"ln0": 0, "ln1": UPDATES["ssm"], "rms0": UPDATES["mlp0"], "rms1": UPDATES["attn"]}

        block = ctx.enter_context(nc.Block())

        @block.sync
        def _(sp):
            def load(dst, src, name):
                sp.dma_start(dst, src).then_inc(s[name], 16)

            def kp(ap, n):
                return ap.rearrange("(c p) n -> p c n", p=P)

            load(cond[:, :, :], kp(t["cond"], B), "cond_in")
            for c in range(C):
                load(x[:, c, :, :], t["x"][:, c * P:(c + 1) * P, :].rearrange("b p t -> p b t"), "x_in")
            load(mod_w[:, 0], kp(t["mamba_w"], 0), "modw_in")
            load(mod_w[:, 1], kp(t["mlp_w"], 0), "modw_in")
            load(cond_w[:, 0], kp(t["shift_w"], 0), "modw_in")
            load(cond_w[:, 1], kp(t["scale_w"], 0), "modw_in")
            for k, name in enumerate(("mamba_b", "mlp_b")):
                load(mod_b[:, k, :], t[name], "modw_in")
            for k, name in enumerate(("shift_b", "scale_b")):
                load(cond_b[:, k, :], t[name], "modw_in")
            load(norm_w[:, :], t["norm_w"], "modw_in")
            load(b_up1[:, :], t["up1_b"], "norm_in")
            load(b_down1[:, :], t["down1_b"], "norm_in")
            load(b_proj[:, :], t["proj_b"], "norm_in")

            for n, (d, b) in enumerate(BDS):
                pre = ("fwd_", "bwd_")[d]
                if b == 0:
                    if n:
                        sp.wait_ge(s["tile_full"], first[f"bc{n - 1}"] + 2)
                        sp.wait_ge(s["decay_ready"], n * HALVES * DS)
                        sp.wait_ge(s["skip_ready"], n * NI)
                        sp.wait_ge(s["tile_full"], first[f"out{n - 1}.1"] + C)
                    load(in_w, kp(t[pre + "in_w"], 0), "ssm_w_in")
                    load(xproj_w, kp(t[pre + "xproj_w"], 0), "ssm_w_in")
                    load(out_w, kp(t[pre + "out_w"], 0), "ssm_w_in")
                    load(a_neg[:, :, :], kp(t[pre + "A_log"], 0), "ssm_small_in")
                    load(dt_bias[:, :], t[pre + "dt_bias"], "ssm_small_in")
                    load(d_skip[:, :], t[pre + "D"], "ssm_small_in")
                sp.wait_ge(s["bc_rows_ready"], 2 * (n + 1))
                sp.dma_start(bc_dram[n], bc_rows[:, :]).then_inc(s["bc_out"], 16)
                sp.wait_ge(s["bc_out"], 16 * (n + 1))
                for hi, half in enumerate(half_order(d)):
                    base = (n * HALVES + hi) * DS

                    def row_pair(pair, k, row):
                        if row == 0:
                            sp.wait_ge(s["u_ready"], pair * 2 + (base + 2))
                        else:
                            sp.wait_ge(s["prod_done"], pair * 2 + (base + 2))
                        src = bc_dram[n, bass.ds(pair * 2 + row * DS, 2), tok(half)]
                        sp.dma_start(bc[:, k, row], src.partition_broadcast(P))\
                          .then_inc(s[f"{'bc'[row]}_in_{k}"], 16)

                    row_pair(0, 0, 0)
                    with sp.Fori(0, DS // 4 - 1) as i:
                        for k in range(2):
                            row_pair(i * 2 + (k + 1), 1 - k, 0)
                            row_pair(i * 2 + k, k, 1)
                    row_pair(DS // 2 - 1, 1, 0)
                    row_pair(DS // 2 - 2, 0, 1)
                    row_pair(DS // 2 - 1, 1, 1)
            for k, name in enumerate(("mlp_w1", "mlp_w2")):
                load(w_up0[:, k], kp(t[name], 0), "mlp0_in")
            load(w_down0, kp(t["mlp_w3"], 0), "mlp0_in")
            sp.wait_ge(s["pad_zero"], 1)
            load(mask_i[:, :, :], t["mask"].rearrange("(a b) n -> a b n", a=1), "mask_in")
            for k in range(2):
                load(qk_w[:, k], kp(t["qkv_w"][:, k * DM:(k + 1) * DM], 0), "attn_w_in")
            for c in range(C):
                src = t["qkv_w"][c * P:(c + 1) * P, 2 * DM:3 * DM]
                dst = v_w[:, c].rearrange("p g (j e) -> p (g j) e", e=HP)[:, :, 0:HD]
                load(dst, src.rearrange("p (h e) -> p h e", e=HD), "attn_w_in")
            pr = t["proj_w"].rearrange("(g j e) n -> j e g n", j=4, e=HD)
            for j in range(4):
                load(proj_w[32 * j:32 * j + HD], pr[j], "attn_w_in")
            load(w_up1, kp(t["up1_w"], 0), "mlp1_in")
            load(w_down1, kp(t["down1_w"], 0), "mlp1_in")
            for b in range(B):
                sp.wait_ge(s["lo_ready"], b + 1)
                for a in range(PARTS):
                    for w in range(2):
                        sp.dma_start(qk_dram[b, a, w].rearrange("(c p) t -> p c t", p=P), qk_parts[:, a, w])\
                          .then_inc(s["qk_out"], 16)
            sp.wait_ge(s["qk_out"], 16 * 2 * PARTS * B)
            for u in range(B * HG):
                b, hg = divmod(u, HG)
                if u == 0:
                    sp.wait_ge(s["ones_set"], 1)
                if u >= 2:
                    sp.wait_ge(s["s2_full"], (u - 1) * 2 * BLOCK)
                for w, parts in enumerate((Q_PARTS, K_PARTS)):
                    for r, a in enumerate(parts):
                        rows = qk_dram[b, a, w, hg * 4 * HD:(hg + 1) * 4 * HD, :]
                        sp.dma_start(stack[r * HD:(r + 1) * HD, u % 2, w], rows.rearrange("(j e) t -> e j t", e=HD))\
                          .then_inc(s[f"stack_in_{u % 2}"], 16)
                sp.dma_start(stack[ONE_ROW:ONE_ROW + 1, u % 2, 1],
                             mask_b[:, b:b + 1, :].to_broadcast([1, 4, L])).then_inc(s[f"stack_in_{u % 2}"], 16)
            for q in range(CHUNKS):
                b, half = divmod(q, HALVES)
                sp.wait_ge(s["x_updated"], UPDATES["attn"] + C * (q + 1))
                for c in range(C):
                    sp.dma_start(t["out"][b, c * P:(c + 1) * P, tok(half)], x[:, c, b, tok(half)])\
                      .then_inc(s["store_out"], 16)
            sp.wait_ge(s["store_out"], 16 * CHUNKS * C)

        @block.gpsimd
        def _(pool):
            pool.memset(ident[:, :], 0.0).then_inc(s["const_ready"], 1)
            pool.memset(sum_sel[:, :], 0.0).then_inc(s["const_ready"], 1)
            pool.memset(ones[:, :], 1.0).then_inc(s["const_ready"], 1)
            pool.memset(mean_w[:, :], 1.0 / DM).then_inc(s["const_ready"], 1)
            pool.memset(ident_b[:, :], 0.0).then_inc(s["const_ready"], 1)
            pool.memset(top_parts[:, :, :, :], 1.0).then_inc(s["const_ready"], 1)
            pool.memset(eps[:, :], 1e-5).then_inc(s["const_ready"], 1)
            pool.wait_ge(s["const_ready"], 7)
            pool.affine_select(out=ident[:, :], in_=ident[:, :], compare_op=ALU.not_equal, fill=1.0,
                               base=0, pattern=[[-1, P]], channel_multiplier=1).then_inc(s["const_ready"], 1)
            sel = sum_sel[:, :].rearrange("p (j e) -> p j e", e=HP)
            pool.affine_select(out=sel, in_=sel, compare_op=ALU.not_equal, fill=1.0, base=-HD,
                               pattern=[[-HP, 4], [0, HP]], channel_multiplier=1).then_inc(s["const_ready"], 1)
            pool.affine_select(out=ident_b[:, :], in_=ident_b[:, :], compare_op=ALU.not_equal, fill=1.0,
                               base=0, pattern=[[-1, P]], channel_multiplier=1).then_inc(s["const_ready"], 1)

            for n, (d, b) in enumerate(BDS):
                pool.wait_ge(s["dt_ready"], n + 1)
                pool.tensor_tensor(dtx, dt_, xs, ALU.mult).then_inc(s["dtx_ready"], 1)
                pool.wait_ge(s["dtx_ready"], n + 1)
                for hi, half in enumerate(half_order(d)):
                    base = (n * HALVES + hi) * DS
                    with pool.Fori(0, DS // 4) as i:
                        for k in range(4):
                            if k % 2 == 0:
                                pool.wait_ge(s[f"b_in_{k // 2}"], i * 16 + (base // 4 + 1) * 16)
                            pool.wait_ge(s["reduce_done"], i * 4 + (base + k + 1))
                            b_row = bc[:, k // 2, 0, k % 2].unsqueeze(1).to_broadcast([P, NI, HALF])
                            pool.tensor_tensor(uh[:, k], dtx[:, :, tok(half)], b_row, ALU.mult)\
                                .then_inc(s["u_ready"], 1)
            pool.wait_ge(s["reduce_done"], SCAN_TILES + 4)
            pool.memset(arena[:, R_DA + 1024:R_DA + 3072], 0.0).then_inc(s["pad_zero"], 1)

        @block.scalar
        def _(act):
            def norm(name):
                k = NORMS.index(name)
                off = CHUNKS * k
                centred = name.startswith("ln")
                tile0 = first[name] + (CHUNKS if centred else 0)
                for q in range(CHUNKS):
                    b, half = divmod(q, HALVES)
                    src = (h if centred else x)[:, :, b, tok(half)]
                    if centred:
                        act.wait_ge(s["centred"], (CHUNKS * k + q + 1) * C)
                    else:
                        act.wait_ge(s["x_updated"], BEFORE[name])
                    if q >= 2:
                        act.wait_ge(s["tile_full"], tile0 + q - 1)
                    act.activation(sq[:, q % 2], src, ACT.Square).then_inc(s["squared"], 1)
                    if q >= 1:
                        std(name, k, q - 1, tile0)
                std(name, k, CHUNKS - 1, tile0)

            def std(name, k, q, tile0):
                act.wait_ge(s["tile_full"], tile0 + q + 1)
                if q >= 2:
                    act.wait_ge(s["normed"], CHUNKS * k + q - 1)
                act.activation(rstd[:, q % 2], bank(tile0 + q), ACT.Sqrt,
                               bias=(eps[:, 0:1] if name.startswith("ln") else 0.0))\
                   .then_inc(s["tile_free_act"], 1)

            act.wait_ge(s["cond_in"], 16)
            act.activation(cond_silu[:, :, :], cond[:, :, :], ACT.Silu).then_inc(s["cond_silu_ready"], 1)
            act.wait_ge(s["const_ready"], 10)
            act.wait_ge(s["x_in"], 32)
            norm("ln0")

            for n, (d, b) in enumerate(BDS):
                if b == 0:
                    act.wait_ge(s["ssm_small_in"], 48 * (d + 1))
                    act.activation(a_neg[:, :, :], a_neg[:, :, :], ACT.Exp).then_inc(s["a_exp"], 1)
                if n:
                    act.wait_ge(s["reduce_done"], (n * HALVES) * DS + 4)
                    act.wait_ge(s["tile_full"], first[f"out{n - 1}.1"] + C)
                for m in range(16):
                    g = first[f"xs{n}"] + m
                    dst = (xs, zs)[m // 8][:, m % 8 // HALVES, tok(m % HALVES)]
                    act.wait_ge(s["tile_full"], g + 1)
                    act.activation(dst, bank(g), ACT.Silu).then_inc(s["tile_free_act"], 1)
                for m in range(8):
                    g = first[f"dt{n}"] + m
                    f, half = divmod(m, HALVES)
                    act.wait_ge(s["tile_full"], g + 1)
                    act.activation(dt_[:, f, tok(half)], bank(g), ACT.Identity, bias=dt_bias[:, f:f + 1])\
                       .then_inc(s["tile_free_act"], 1)
                act.wait_ge(s["tile_free_act"], eaten(first[f"dt{n}"] + 7, "a"))
                act.activation(dtx, dt_, ACT.Abs).then_inc(s["exp_step"], 1)
                act.wait_ge(s["exp_step"], 3 * n + 1)
                act.activation(dtx, dtx, ACT.Exp, scale=-1.0).then_inc(s["exp_step"], 1)
                act.wait_ge(s["exp_step"], 3 * n + 2)
                act.activation(dtx, dtx, ACT.Ln, bias=1.0).then_inc(s["exp_step"], 1)
                act.wait_ge(s["dtx_ready"], n + 1)
                for f in range(NI):
                    act.activation(xs[:, f], xs[:, f], ACT.Copy, scale=d_skip[:, f:f + 1])\
                       .then_inc(s["skip_ready"], 1)
                act.wait_ge(s["a_ready"], d + 1)
                for hi, half in enumerate(half_order(d)):
                    base = (n * HALVES + hi) * DS

                    def save(st, k):
                        act.wait_ge(s["scan_done"], st + (base + 3))
                        at = 0 if d == 1 else HALF - 1
                        act.activation(carry[:, bass.ds(st, 1), :].rearrange("p a b -> p (a b)"),
                                       uh[:, k, :, at], ACT.Copy).then_inc(s["carry_saved"], 1)

                    def decays(st, k, saves):
                        act.wait_ge(s["scan_done"], st + (base + 1))
                        if saves:
                            save(st - 2, (k + 2) % 4)
                        for f in range(NI):
                            e = act.activation(decay[:, k % 2, f], dt_[:, f, tok(half)], ACT.Exp,
                                               scale=a_neg[:, f, bass.ds(st, 1)])
                        e.then_inc(s["decay_ready"], 1)

                    for k in range(4):
                        decays(k, k, hi == 0 and k >= 2)
                    with act.Fori(1, DS // 4) as i:
                        for k in range(4):
                            decays(i * 4 + k, k, hi == 0)
                    if hi == 0:
                        save(DS - 2, 2)
                        save(DS - 1, 3)

            def mlp(name, n_hidden, gbuf, bias):
                chunk0 = 0 if name == "ln1" else CHUNKS
                silu0 = 0 if name == "ln1" else CHUNKS * MH0 // P
                for q in range(CHUNKS):
                    if q >= 2:
                        act.wait_ge(s["tile_full"], first[f"down{name}.{q - 2}"] + C)
                    for m in range(n_hidden):
                        g = first[f"up{name}.{q}"] + 2 * m
                        act.wait_ge(s["tile_full"], g + 1)
                        act.activation(gbuf[:, q % 2, m], bank(g), ACT.Silu,
                                       bias=(bias[:, m:m + 1] if bias is not None else 0.0))\
                           .then_inc(s["tile_free_act"], 1)

            norm("ln1")
            mlp("ln1", MH0 // P, g0, None)
            norm("rms0")
            act.wait_ge(s["any_full"], 1)
            act.activation(q_scale[:, :], psum[:, 0, 0:B], ACT.Copy, scale=HD ** -0.5)\
               .then_inc(s["q_scale_ready"], 1)
            act.wait_ge(s["q_scale_ready"], 1)
            for b in range(B):
                if b:
                    act.wait_ge(s["lo_ready"], b)
                for m in range(2 * C * HALVES):
                    g = first[f"qk{b}"] + m
                    w, r = divmod(m, C * HALVES)
                    c, half = divmod(r, HALVES)
                    act.wait_ge(s["tile_full"], g + 1)
                    act.activation(qk[:, w, c, tok(half)], bank(g), ACT.Copy,
                                   scale=(1.0 if w else q_scale[:, b:b + 1])).then_inc(s["tile_free_act"], 1)
                act.wait_ge(s["tile_free_act"], eaten(first[f"qk{b}"] + 2 * C * HALVES - 1, "a"))
                if b:
                    act.wait_ge(s["qk_out"], 16 * 2 * PARTS * b)
                act.activation(qk_parts[:, 0], qk, ACT.Copy).then_inc(s["hi_ready"], 1)
                for kt in range(QT):
                    g = first[f"v{b}"] + kt
                    act.wait_ge(s["tile_full"], g + 1)
                    act.activation(v_aug[:, b, kt].rearrange("p g e -> p (g e)"), bank(g), ACT.Copy)\
                       .then_inc(s["tile_free_act"], 1)
                act.wait_ge(s["rest_ready"], b + 1)
                act.activation(qk_parts[:, 1], qk, ACT.Copy).then_inc(s["mid_ready"], 1)

            def copy_attn(v):
                act.wait_ge(s["pv_done"], (v + 1) * BLOCK)
                if v:
                    act.wait_ge(s["attn_ready"], v)
                act.activation(attn_sb[:, 0], psum[:, 4], ACT.Copy).then_inc(s["attn_copied"], 1)

            for v in range(B * HG * HALVES):
                u, qh = divmod(v, HALVES)
                if qh == 0:
                    for j in range(4):
                        act.wait_ge(s["rows_full_0"], u * 4 + j + 1)
                        act.activation(stack[ONE_ROW:ROWS, u % 2, 0, j, tok(0)], psum[ONE_ROW:ROWS, 5], ACT.Copy)\
                           .then_inc(s["rows_ready_0"], 1)
                for m in range(BLOCK):
                    w = v * BLOCK + m
                    act.wait_ge(s["s2_full"], w + 1)
                    if w >= 3:
                        act.wait_ge(s["pv_done"], w - 2)
                    sl = 2 * (w % 2)
                    act.activation(probs[:, w % 3], psum[:, sl:sl + 2, :], ACT.Exp).then_inc(s["probs_ready"], 1)
                    if m == 0 and v:
                        copy_attn(v - 1)
            copy_attn(B * HG * HALVES - 1)
            norm("rms1")
            mlp("rms1", MH1 // P, g1, b_up1)

        @block.vector
        def _(dve):
            dve.memset(carry[:, :, :], 0.0).then_inc(s["reduce_done"], 4)
            dve.memset(top[:, :, :], 0.0).then_inc(s["scan_done"], 2)
            dve.memset(row_max[:, :, :, :], 0.0).then_inc(s["prod_done"], 4)
            dve.memset(attn_sb[:, :, :], 0.0).then_inc(s["u_ready"], 4)

            dve.wait_ge(s["modw_in"], 16 * 9)
            for k in range(2):
                g = first["mods"] + k
                dve.wait_ge(s["tile_full"], g + 1)
                dve.tensor_tensor(mods[:, k], bank(g)[:, 0:6 * B].rearrange("p (a b) -> p a b", b=B),
                                  mod_b[:, k, :].unsqueeze(2).to_broadcast([P, 6, B]), ALU.add)\
                   .then_inc(s["tile_free_dve"], 1)
            dve.wait_ge(s["tile_free_dve"], 2)
            dve.tensor_scalar(mods[:, :, C:2 * C, :], mods[:, :, C:2 * C, :], 1.0, None, ALU.add)\
               .then_inc(s["mods_ready"], 1)
            g = first["mods"] + 2
            dve.wait_ge(s["tile_full"], g + 1)
            dve.tensor_tensor(cmod[:, :, :, :], bank(g)[:, 0:2 * C * B].rearrange("p (k c b) -> p k c b", k=2, b=B),
                              cond_b[:, :, :].unsqueeze(3).to_broadcast([P, 2, C, B]), ALU.add)\
               .then_inc(s["tile_free_dve"], 1)
            dve.wait_ge(s["tile_free_dve"], 3)
            dve.tensor_scalar(cmod[:, 1], cmod[:, 1], 1.0, 0.1, ALU.add, ALU.max).then_inc(s["mods_step"], 1)
            dve.wait_ge(s["mods_step"], 1)
            dve.scalar_tensor_tensor(cmod[:, 1], cmod[:, 1], 10.0,
                                     norm_w[:, :].unsqueeze(2).to_broadcast([P, C, B]), ALU.min, ALU.mult)\
               .then_inc(s["mods_ready"], 1)
            dve.wait_ge(s["mods_ready"], 2)

            def norm(name):
                k = NORMS.index(name)
                centred = name.startswith("ln")
                tile0 = first[name] + (CHUNKS if centred else 0)
                if BEFORE[name]:
                    dve.wait_ge(s["x_updated"], BEFORE[name])
                if centred:
                    for q in range(CHUNKS):
                        b, half = divmod(q, HALVES)
                        g = first[name] + q
                        dve.wait_ge(s["tile_full"], g + 1)
                        for c in range(C):
                            o = dve.tensor_tensor(h[:, c, b, tok(half)], x[:, c, b, tok(half)], bank(g),
                                                  ALU.subtract).then_inc(s["centred"], 1)
                for q in range(CHUNKS):
                    b, half = divmod(q, HALVES)
                    Q = CHUNKS * k + q
                    r = rstd[:, q % 2]
                    dve.wait_ge(s["tile_free_act"], eaten(tile0 + q, "a"))
                    if not centred:
                        dve.tensor_scalar(r, r, 1e-6, None, ALU.max).then_inc(s["mid_step"], 1)
                        dve.wait_ge(s["mid_step"], CHUNKS * (k - 2) + q + 1)
                    dve.reciprocal(r, r).then_inc(s["rstd_ready"], 1)
                    dve.wait_ge(s["rstd_ready"], Q + 1)
                    hq = h[:, :, b, tok(half)]
                    src = hq if centred else x[:, :, b, tok(half)]
                    dve.tensor_tensor(hq, src, r.unsqueeze(1).to_broadcast([P, C, HALF]), ALU.mult)\
                       .then_inc(s["normed"], 1)
                    dve.wait_ge(s["normed"], Q + 1)
                    for c in range(C):
                        if centred:
                            mul, add = mods[:, k, C + c, b:b + 1], mods[:, k, c, b:b + 1]
                        else:
                            mul, add = cmod[:, 1, c, b:b + 1], cmod[:, 0, c, b:b + 1]
                        dve.tensor_scalar(h[:, c, b, tok(half)], h[:, c, b, tok(half)], mul, add,
                                          ALU.mult, ALU.add).then_inc(s["h_ready"], 1)

            norm("ln0")

            for n, (d, b) in enumerate(BDS):
                for m in range(HALVES):
                    g = first[f"bc{n}"] + m
                    dve.wait_ge(s["tile_full"], g + 1)
                    if n and m == 0:
                        dve.wait_ge(s["bc_out"], 16 * n)
                    dve.tensor_copy(bc_rows[:, tok(m)], bank(g)).then_inc(s["bc_rows_ready"], 1)
                if b == 0:
                    dve.wait_ge(s["a_exp"], d + 1)
                    dve.tensor_scalar(a_neg[:, :, :], a_neg[:, :, :], -1.0, None, ALU.mult).then_inc(s["a_ready"], 1)
                dve.wait_ge(s["exp_step"], 3 * n + 3)
                dve.scalar_tensor_tensor(dt_, dt_, 0.0, dtx, ALU.max, ALU.add).then_inc(s["dt_ready"], 1)

                rev = d == 1

                def along(ap):
                    return ap[:, ::-1] if rev else ap

                for hi, half in enumerate(half_order(d)):
                    base = (n * HALVES + hi) * DS

                    def scan(st, k):
                        dve.wait_ge(s["decay_ready"], st + (base + 1))
                        dve.wait_ge(s["u_ready"], st + (base + 5))
                        for f in range(NI):
                            start = carry[:, bass.ds(st, 1), f] if hi else 0.0
                            o = dve.tensor_tensor_scan(along(uh[:, k, f]), along(decay[:, k % 2, f]),
                                                       along(uh[:, k, f]), start, op0=ALU.mult, op1=ALU.add)
                        o.then_inc(s["scan_done"], 1)

                    def weigh(st, k):
                        dve.wait_ge(s["scan_done"], st + (base + 3))
                        if hi == 0:
                            dve.wait_ge(s["carry_saved"], st + (DS * n + 1))
                        if k % 2 == 0:
                            dve.wait_ge(s[f"c_in_{k // 2}"], (base // 4 + 1) * 16 + (st - k) * 4)
                        c_row = bc[:, k // 2, 1, k % 2].unsqueeze(1).to_broadcast([P, NI, HALF])
                        dve.tensor_tensor(uh[:, k], uh[:, k], c_row, ALU.mult).then_inc(s["prod_done"], 1)

                    if hi:
                        dve.wait_ge(s["carry_saved"], DS * (n + 1))
                    scan(0, 0)
                    with dve.Fori(0, DS // 4 - 1) as i:
                        for k in range(4):
                            scan(i * 4 + (k + 1), (k + 1) % 4)
                            weigh(i * 4 + k, k)
                    for k in range(4):
                        if k < 3:
                            scan(DS - 4 + k + 1, k + 1)
                        weigh(DS - 4 + k, k)
                    dve.wait_ge(s["reduce_done"], base + DS + 4)
                    dve.tensor_tensor(zs[:, :, tok(half)], psum[:, 0:4, :], zs[:, :, tok(half)], ALU.mult)\
                       .then_inc(s["gated"], 1)
                    for c in range(C):
                        g = first[f"out{n}.{hi}"] + c
                        xc = x[:, c, b, tok(half)]
                        dve.wait_ge(s["tile_full"], g + 1)
                        dve.scalar_tensor_tensor(xc, bank(g), mods[:, 0, 2 * C + c, b:b + 1], xc, ALU.mult, ALU.add)\
                           .then_inc(s["x_updated"], 1)

            def mlp(name, n_hidden, gbuf, up_bias, finish, done0):
                for q in range(CHUNKS + 1):
                    if q < CHUNKS:
                        for m in range(n_hidden):
                            g = first[f"up{name}.{q}"] + 2 * m + 1
                            gm = gbuf[:, q % 2, m]
                            dve.wait_ge(s["tile_full"], g + 1)
                            dve.wait_ge(s["tile_free_act"], eaten(g - 1, "a"))
                            add = up_bias[:, n_hidden + m:n_hidden + m + 1] if up_bias is not None else 0.0
                            dve.scalar_tensor_tensor(gm, bank(g), add, gm, ALU.add, ALU.mult)\
                               .then_inc(s["tile_free_dve"], 1)
                    if q:
                        b, half = divmod(q - 1, HALVES)
                        for c in range(C):
                            g = first[f"down{name}.{q - 1}"] + c
                            xc = x[:, c, b, tok(half)]
                            dve.wait_ge(s["tile_full"], g + 1)
                            finish(xc, bank(g), c, b).then_inc(s["x_updated"], 1)

            dve.wait_ge(s["mask_in"], 16)
            dve.tensor_scalar(mask_f[:, :, :], mask_i[:, :, :], 0.0, None, ALU.not_equal).then_inc(s["mask_step"], 1)
            dve.wait_ge(s["mask_step"], 1)
            dve.tensor_reduce(any_row[:, :], mask_f[:, :, :], axis=AX.X, op=ALU.max).then_inc(s["mask_step"], 1)
            dve.tensor_scalar(mask_d[:, :, :], mask_f[:, :, :], -1.0, BIG, ALU.add, ALU.mult)\
               .then_inc(s["mask_step"], 1)
            dve.wait_ge(s["mask_step"], 3)
            for b in range(B):
                dve.tensor_scalar(mask_b[:, b, :], mask_d[:, b, :], any_row[:, b:b + 1], None, ALU.mult)\
                   .then_inc(s["mask_ready"], 1)

            norm("ln1")
            mlp("ln1", MH0 // P, g0, None,
                lambda xc, y, c, b: dve.scalar_tensor_tensor(xc, y, mods[:, 1, 2 * C + c, b:b + 1], xc,
                                                             ALU.mult, ALU.add), UPDATES["ssm"])
            norm("rms0")
            for b in range(B):
                dve.wait_ge(s["hi_ready"], b + 1)
                dve.tensor_tensor(qk, qk, qk_parts[:, 0], ALU.subtract).then_inc(s["rest_ready"], 1)
                dve.wait_ge(s["mid_ready"], b + 1)
                dve.tensor_tensor(qk_parts[:, 2], qk, qk_parts[:, 1], ALU.subtract).then_inc(s["lo_ready"], 1)
                dve.wait_ge(s["tile_free_act"], eaten(first[f"v{b}"] + QT - 1, "a"))
                dve.memset(v_aug[:, b].rearrange("p t g (j e) -> p t (g j) e", e=HP)[:, :, :, HD:HD + 1], 1.0)\
                   .then_inc(s["v_ready"], 1)
            dve.wait_ge(s["qk_out"], 16 * 2 * PARTS * B)
            dve.memset(arena[ONE_ROW:ROWS, R_XS:R_XS + 8192], TWO_ONES).then_inc(s["ones_set"], 1)

            def score_max(w):
                u, m = divmod(w, 4 * QT * HALVES)
                j, r = divmod(m, QT * HALVES)
                qt, kh = divmod(r, HALVES)
                dve.wait_ge(s["scores_full"], w + 1)
                if m == 0 and u:
                    dve.wait_ge(s["top_ready"], 4 * u)
                dve.tensor_reduce(row_max[:, qt, j, kh:kh + 1], psum[:, 5 + w % 2, :], axis=AX.X, op=ALU.max)\
                   .then_inc(s["scores_free"], 1)

            def finish_max(u):
                dve.wait_ge(s["scores_free"], (u + 1) * 4 * QT * HALVES)
                if u:
                    dve.wait_ge(s["rows_full_0"], u * 4)
                    dve.wait_ge(s["rows_full_1"], u * 4)
                dve.tensor_reduce(top[:, :, :], row_max[:, :, :, :], axis=AX.X, op=ALU.max).then_inc(s["top_ready"], 1)
                dve.wait_ge(s["top_ready"], 4 * u + 1)
                dve.tensor_scalar(top_parts[:, :, :, 1], top[:, :, :], -1.0, None, ALU.mult)\
                   .then_inc(s["top_ready"], 1)
                dve.wait_ge(s["top_ready"], 4 * u + 2)
                dve.scalar_tensor_tensor(top_rest[:, :, :], top[:, :, :], -1.0, top_parts[:, :, :, 1],
                                         ALU.mult, ALU.subtract).then_inc(s["max_step"], 1)
                dve.wait_ge(s["max_step"], u + 1)
                dve.tensor_copy(top_parts[:, :, :, 2], top_rest[:, :, :]).then_inc(s["top_ready"], 1)
                dve.wait_ge(s["top_ready"], 4 * u + 3)
                dve.tensor_tensor(top_parts[:, :, :, 3], top_rest[:, :, :], top_parts[:, :, :, 2], ALU.subtract)\
                   .then_inc(s["top_ready"], 1)
                for j in range(4):
                    dve.wait_ge(s["rows_full_1"], u * 4 + j + 1)
                    dve.tensor_copy(stack[ONE_ROW:ROWS, u % 2, 0, j, tok(1)], psum[ONE_ROW:ROWS, 6])\
                       .then_inc(s["rows_ready_1"], 1)

            def normalise(v):
                u, qh = divmod(v, HALVES)
                b, hg = divmod(u, HG)
                dve.wait_ge(s["sums_full"], v + 1)
                dve.reciprocal(attn_sb[:, 1], psum[:, 7]).then_inc(s["recip_ready"], 1)
                dve.wait_ge(s["recip_ready"], v + 1)
                dve.tensor_tensor(attnT[b][:, hg, tok(qh)], attn_sb[:, 0], attn_sb[:, 1], ALU.mult)\
                   .then_inc(s["attn_ready"], 1)

            for w in range(4 * QT * HALVES):
                score_max(w)
            finish_max(0)
            for v in range(B * HG * HALVES):
                if v // 2 + 1 < B * HG:
                    for m in range(4 * QT):
                        score_max((v + 2) * 4 * QT + m)
                        if m == 8 and v:
                            normalise(v - 1)
                    if v % 2:
                        finish_max(v // 2 + 1)
                elif v:
                    normalise(v - 1)
            normalise(B * HG * HALVES - 1)
            for m in range(C * CHUNKS):
                q, c = divmod(m, C)
                b, half = divmod(q, HALVES)
                g = first["proj"] + m
                xc = x[:, c, b, tok(half)]
                dve.wait_ge(s["tile_full"], g + 1)
                dve.scalar_tensor_tensor(xc, bank(g), b_proj[:, c:c + 1], xc, ALU.add, ALU.add)\
                   .then_inc(s["x_updated"], 1)
            norm("rms1")
            mlp("rms1", MH1 // P, g1, b_up1,
                lambda xc, y, c, b: dve.scalar_tensor_tensor(xc, y, b_down1[:, c:c + 1], xc, ALU.add, ALU.add),
                UPDATES["attn"])

        @block.tensor
        def _(pe):
            def product(dst, pairs, last=None):
                for k, (lhsT, rhs) in enumerate(pairs):
                    o = pe.matmul(dst, lhsT, rhs, start=k == 0, stop=k == len(pairs) - 1)
                return o

            def norm(name):
                k = NORMS.index(name)
                centred = name.startswith("ln")
                if BEFORE[name]:
                    pe.wait_ge(s["x_updated"], BEFORE[name])
                if centred:
                    for q in range(CHUNKS):
                        b, half = divmod(q, HALVES)
                        dst = take(pe, first[name] + q)
                        product(dst, [(mean_w[:, :], x[:, c, b, tok(half)]) for c in range(C)])\
                            .then_inc(s["tile_full"], 1)
                tile0 = first[name] + (CHUNKS if centred else 0)
                for q in range(CHUNKS):
                    pe.wait_ge(s["squared"], CHUNKS * k + q + 1)
                    dst = take(pe, tile0 + q)
                    product(dst, [(mean_w[:, :], sq[:, q % 2, c]) for c in range(C)]).then_inc(s["tile_full"], 1)

            pe.wait_ge(s["const_ready"], 10)
            pe.wait_ge(s["modw_in"], 16 * 9)
            for k in range(2):
                dst = take(pe, first["mods"] + k)
                for m in range(6):
                    o = product(dst[:, m * B:(m + 1) * B],
                                [(mod_w[:, k, c, m * P:(m + 1) * P], cond[:, c, :]) for c in range(C)])
                o.then_inc(s["tile_full"], 1)
            pe.wait_ge(s["cond_silu_ready"], 1)
            dst = take(pe, first["mods"] + 2)
            for k in range(2):
                for m in range(C):
                    r = (k * C + m) * B
                    o = product(dst[:, r:r + B],
                                [(cond_w[:, k, c, m * P:(m + 1) * P], cond_silu[:, c, :]) for c in range(C)])
            o.then_inc(s["tile_full"], 1)
            pe.wait_ge(s["x_in"], 32)
            norm("ln0")
            pe.wait_ge(s["h_ready"], CHUNKS * C)

            for n, (d, b) in enumerate(BDS):
                if b == 0:
                    pe.wait_ge(s["ssm_w_in"], 16 * 3 * (d + 1))
                for m in range(16):
                    path, r = divmod(m, 8)
                    f, half = divmod(r, HALVES)
                    dst = take(pe, first[f"xs{n}"] + m)
                    pairs = []
                    for c in range(C):
                        w = in_w[:, c, path * DI + f * P:path * DI + (f + 1) * P]
                        pairs.append((w, h[:, c, b, tok(half)]))
                    product(dst, pairs).then_inc(s["tile_full"], 1)
                pe.wait_ge(s["tile_free_act"], eaten(first[f"xs{n}"] + 7, "a"))
                for m in range(10):
                    f, half = divmod(m, HALVES)
                    dst = take(pe, first[f"dt{n}"] + m)
                    product(dst, [(xproj_w[:, c, f * P:(f + 1) * P], xs[:, c, tok(half)]) for c in range(NI)])\
                        .then_inc(s["tile_full"], 1)

                for hi, half in enumerate(half_order(d)):
                    base = (n * HALVES + hi) * DS

                    def reduce(rhs, start, stop):
                        for f in range(NI):
                            o = pe.matmul(psum[:, f, :], ident[:, :], rhs[:, f, :], start=start, stop=stop)
                        return o

                    pe.wait_ge(s["skip_ready"], NI * (n + 1))
                    if n or hi:
                        pe.wait_ge(s["gated"], n * HALVES + hi)
                    reduce(xs[:, :, tok(half)], True, False)
                    with pe.Fori(0, DS // 4 - 1) as i:
                        for k in range(4):
                            pe.wait_ge(s["prod_done"], i * 4 + (base + k + 5))
                            reduce(uh[:, k], False, False).then_inc(s["reduce_done"], 1)
                    for k in range(4):
                        pe.wait_ge(s["prod_done"], base + DS - 4 + k + 5)
                        reduce(uh[:, k], False, k == 3).then_inc(s["reduce_done"], 1)
                    pe.wait_ge(s["gated"], n * HALVES + hi + 1)
                    for c in range(C):
                        dst = take(pe, first[f"out{n}.{hi}"] + c)
                        product(dst, [(out_w[:, f, c * P:(c + 1) * P], zs[:, f, tok(half)]) for f in range(NI)])\
                            .then_inc(s["tile_full"], 1)

            def mlp(name, n_hidden, gbuf, weights, down):
                for q in range(CHUNKS + 1):
                    if q < CHUNKS:
                        b, half = divmod(q, HALVES)
                        for m in range(2 * n_hidden):
                            hidden, which = divmod(m, 2)
                            dst = take(pe, first[f"up{name}.{q}"] + m)
                            product(dst, [(weights(c, which, hidden), h[:, c, b, tok(half)]) for c in range(C)])\
                                .then_inc(s["tile_full"], 1)
                    if q:
                        pe.wait_ge(s["tile_free_dve"], eaten(first[f"up{name}.{q - 1}"] + 2 * n_hidden - 1, "d"))
                        for c in range(C):
                            dst = take(pe, first[f"down{name}.{q - 1}"] + c)
                            product(dst, [(down[:, m, c * P:(c + 1) * P], gbuf[:, (q - 1) % 2, m])
                                          for m in range(n_hidden)]).then_inc(s["tile_full"], 1)

            norm("ln1")
            pe.wait_ge(s["mlp0_in"], 48)
            pe.wait_ge(s["h_ready"], 2 * CHUNKS * C)
            mlp("ln1", MH0 // P, g0, lambda c, which, m: w_up0[:, which, c, m * P:(m + 1) * P], w_down0)
            norm("rms0")
            pe.wait_ge(s["attn_w_in"], 16 * 8)
            pe.wait_ge(s["h_ready"], 3 * CHUNKS * C)
            pe.wait_ge(s["mask_ready"], B)
            pe.matmul(psum[:, 0, 0:B], ones[0:1, :], any_row[:, :], start=True, stop=True).then_inc(s["any_full"], 1)
            for b in range(B):
                for m in range(2 * C * HALVES):
                    w, r = divmod(m, C * HALVES)
                    f, half = divmod(r, HALVES)
                    dst = take(pe, first[f"qk{b}"] + m)
                    product(dst, [(qk_w[:, w, c, f * P:(f + 1) * P], h[:, c, b, tok(half)]) for c in range(C)])\
                        .then_inc(s["tile_full"], 1)
                for kt in range(QT):
                    dst = take(pe, first[f"v{b}"] + kt)
                    product(dst, [(h[:, c, b, kt * P:(kt + 1) * P], v_w[:, c].rearrange("p g e -> p (g e)"))
                                  for c in range(C)]).then_inc(s["tile_full"], 1)
            pe.wait_ge(s["tile_free_act"], eaten(first[f"v{B - 1}"] + QT - 1, "a"))
            pe.wait_ge(s["v_ready"], B)

            def scores(w):
                u, m = divmod(w, 4 * QT * HALVES)
                j, r = divmod(m, QT * HALVES)
                qt, kh = divmod(r, HALVES)
                if m == 0:
                    pe.wait_ge(s[f"stack_in_{u % 2}"], LOADS * (u // 2 + 1))
                    if u:
                        pe.wait_ge(s["rows_ready_0"], 4 * u)
                        pe.wait_ge(s["rows_ready_1"], 4 * u)
                if m >= 2:
                    pe.wait_ge(s["scores_free"], w - 1)
                pe.matmul(psum[:, 5 + w % 2, :], stack[0:PLAIN, u % 2, 0, j, qt * P:(qt + 1) * P],
                          stack[0:PLAIN, u % 2, 1, j, tok(kh)], start=True, stop=True)\
                  .then_inc(s["scores_full"], 1)

            def max_rows(u):
                pe.wait_ge(s["top_ready"], 4 * (u + 1))
                for j in range(4):
                    for half in range(HALVES):
                        if j:
                            pe.wait_ge(s[f"rows_ready_{half}"], 4 * u + j)
                        for r in range(4):
                            o = pe.matmul(psum[ONE_ROW:ROWS, 5 + half, r * P:(r + 1) * P],
                                          top_parts[:, half * 4 + r, j, :], ident_b[:, :], start=True, stop=True)
                        o.then_inc(s[f"rows_full_{half}"], 1)

            def scores2(v, m):
                u, qh = divmod(v, HALVES)
                kt, pair = divmod(m, 2)
                w = v * BLOCK + m
                if m == 0:
                    pe.wait_ge(s[f"rows_ready_{qh}"], 4 * (u + 1))
                if w >= 2:
                    pe.wait_ge(s["probs_ready"], w - 1)
                for jj in range(2):
                    j = 2 * pair + jj
                    o = pe.matmul(psum[:, 2 * (w % 2) + jj, :], stack[0:ROWS, u % 2, 1, j, kt * P:(kt + 1) * P],
                                  stack[0:ROWS, u % 2, 0, j, tok(qh)], start=True, stop=True)
                o.then_inc(s["s2_full"], 1)

            def weigh_v(v, m):
                b, hg = divmod(v // HALVES, HG)
                kt, pair = divmod(m, 2)
                w = v * BLOCK + m
                pe.wait_ge(s["probs_ready"], w + 1)
                if v and m == 0:
                    pe.wait_ge(s["attn_copied"], v)
                for jj in range(2):
                    j = 2 * pair + jj
                    o = pe.matmul(psum[32 * j:32 * j + 32, 4, :], v_aug[:, b, kt, hg, 32 * j:32 * j + 32],
                                  probs[:, w % 3, jj], start=kt == 0, stop=kt == QT - 1)
                o.then_inc(s["pv_done"], 1)

            def sums(v):
                pe.wait_ge(s["attn_copied"], v + 1)
                if v:
                    pe.wait_ge(s["recip_ready"], v)
                pe.matmul(psum[:, 7, :], sum_sel[:, :], attn_sb[:, 0], start=True, stop=True)\
                  .then_inc(s["sums_full"], 1)

            for w in range(4 * QT * HALVES):
                scores(w)
            max_rows(0)
            for v in range(B * HG * HALVES):
                more = v // 2 + 1 < B * HG
                for m in range(BLOCK):
                    scores2(v, m)
                    if more:
                        for k in range(2):
                            scores((v + 2) * 4 * QT + 2 * m + k)
                    if m:
                        weigh_v(v, m - 1)
                    if m == 3 and v:
                        sums(v - 1)
                weigh_v(v, BLOCK - 1)
                if v % 2 and more:
                    max_rows(v // 2 + 1)
            sums(B * HG * HALVES - 1)
            pe.wait_ge(s["attn_ready"], B * HG * HALVES)
            for m in range(C * CHUNKS):
                q, c = divmod(m, C)
                b, half = divmod(q, HALVES)
                dst = take(pe, first["proj"] + m)
                product(dst, [(proj_w[:, hg, c * P:(c + 1) * P], attnT[b][:, hg, tok(half)]) for hg in range(HG)])\
                    .then_inc(s["tile_full"], 1)
            norm("rms1")
            pe.wait_ge(s["mlp1_in"], 32)
            pe.wait_ge(s["norm_in"], 48)
            pe.wait_ge(s["h_ready"], 4 * CHUNKS * C)
            mlp("rms1", MH1 // P, g1,
                lambda c, which, m: w_up1[:, c, which * MH1 + m * P:which * MH1 + (m + 1) * P], w_down1)


def kernel(**inputs):
    import numpy as np
    import concourse.bacc as bacc
    from concourse.bass_utils import run_bass_kernel_spmd

    g = {k: np.asarray(v) for k, v in inputs.items()}
    l0, l1 = "L0_cond_", "L1_cond_"

    def lay(a):
        return np.ascontiguousarray(a)

    arrays = {
        "x": lay(g["x"].transpose(0, 2, 1)),
        "cond": lay(g["cond_1024"].T),
        "mask": lay(g["mask_BxS_ik0"]),
        "mamba_w": lay(g[l0 + "adaln_mamba_w"]), "mamba_b": lay(g[l0 + "adaln_mamba_b"]),
        "mlp_w": lay(g[l0 + "adaln_mlp_w"]), "mlp_b": lay(g[l0 + "adaln_mlp_b"]),
        "mlp_w1": lay(g[l0 + "mlp_w1"]), "mlp_w2": lay(g[l0 + "mlp_w2"]), "mlp_w3": lay(g[l0 + "mlp_w3"]),
        "norm_w": lay(g[l1 + "norm_w"]),
        "scale_w": lay(g[l1 + "scale_w"].T), "scale_b": lay(g[l1 + "scale_b"]),
        "shift_w": lay(g[l1 + "shift_w"].T), "shift_b": lay(g[l1 + "shift_b"]),
        "qkv_w": lay(g[l1 + "qkv_w"].T),
        "proj_w": lay(g[l1 + "proj_w"].T), "proj_b": lay(g[l1 + "proj_b"]),
        "up1_w": lay(g[l1 + "mlp_w1"].T), "up1_b": lay(g[l1 + "mlp_b1"]),
        "down1_w": lay(g[l1 + "mlp_w2"].T), "down1_b": lay(g[l1 + "mlp_b2"]),
    }
    for pre in ("fwd_", "bwd_"):
        for name in ("in_w", "xproj_w", "dt_bias", "A_log", "D", "out_w"):
            arrays[pre + name] = lay(g[l0 + pre + name])
    arrays = {k: lay(a.reshape(-1, P).T) if a.ndim == 1 else a for k, a in arrays.items()}

    nc = bacc.Bacc("TRN2", target_bir_lowering=False, num_devices=1)
    t = {k: nc.dram_tensor(f"in_{k}", a.shape, mybir.dt.from_np(a.dtype), kind="ExternalInput").ap()
         for k, a in arrays.items()}
    t["out"] = nc.dram_tensor("out_xT", (B, DM, L), mybir.dt.float32, kind="ExternalOutput").ap()
    build(nc, t)
    r = run_bass_kernel_spmd(nc, [{f"in_{k}": a for k, a in arrays.items()}], core_ids=[0])
    return lay(r.results[0]["out_xT"].transpose(0, 2, 1))
```

```python
import concourse.bass as bass
from concourse import mybir
from contextlib import ExitStack

P = 128
B, L, DM = 2, 1024, 256
DI, DS = 512, 64
HEADS, HD = 16, 16
HP = 32
MH0, MH1 = 512, 1024
C = DM // P
NI = DI // P
HALF = 512
HALVES = L // HALF
CHUNKS = B * HALVES
HG = HEADS // 4
QT = L // P
BIG = 1.0e30
PARTS = 3
Q_PARTS = (0, 0, 1, 0, 2, 1)
K_PARTS = (0, 1, 0, 2, 0, 1)
PLAIN = 6 * HD + 1
ROWS = PLAIN + PARTS
ONE_ROW = 6 * HD
LOADS = 16 * (12 + 1)
TWO_ONES = 1.0 + 2.0 ** -9 - 2.0 ** -16
BLOCK = 2 * QT
UNITS = 2 * B * HALVES
SCAN_TILES = UNITS * DS
STACKS = 3
SCORE_TILES = 4 * QT * HALVES
LEAD = 20
ROW_STEPS = (8, 10, 12, 14)
RECIP_STEPS = (6, 7, 9, 10)
SUMS_STEP = 4
SEGS = 8
ITERS = DS // 4 // SEGS


def build(nc, t):
    F32, I32, BF16 = mybir.dt.float32, mybir.dt.int32, mybir.dt.bfloat16
    ALU, ACT, AX = mybir.AluOpType, mybir.ActivationFunctionType, mybir.AxisListType

    ctx = ExitStack()
    with ctx:
        def sb(name, shape, dt=F32):
            return ctx.enter_context(nc.sbuf_tensor(name, shape, dt))

        def sem(name):
            return ctx.enter_context(nc.semaphore(name))

        arena = sb("arena", [P, 46640])

        def cut(at, *dims):
            n = 1
            for d in dims:
                n *= d
            v = arena[:, at:at + n]
            if len(dims) == 2:
                v = v.rearrange("p (a b) -> p a b", b=dims[1])
            if len(dims) == 3:
                v = v.rearrange("p (a b c) -> p a b c", b=dims[1], c=dims[2])
            if len(dims) == 4:
                v = v.rearrange("p (a b c d) -> p a b c d", b=dims[1], c=dims[2], d=dims[3])
            return v

        R_X, R_H, R_W = 0, 4096, 8192
        R_XS, R_DT, R_DTX, R_ZS = 13824, 17920, 22016, 26112
        R_DA, R_UH, R_BC = 30208, 34320, 42544

        x = cut(R_X, C, B, L)
        h = cut(R_H, C, B, L)
        in_w = cut(R_W, C, 2 * DI)
        xproj_w = cut(R_W + 2048, NI, DI + 2 * DS)
        out_w = cut(R_W + 4608, NI, DM)
        xs = cut(R_XS, 2, NI, HALF)
        dt_ = cut(R_DT, 2, NI, HALF)
        dtx = cut(R_DTX, 2, NI, HALF)
        zs = cut(R_ZS, 2, NI, HALF)
        decay_ends = cut(R_DA, 2, NI, HALF + 2)
        uh_ends = cut(R_UH, 4, NI, HALF + 2)
        decay, uh = decay_ends[:, :, :, 1:HALF + 1], uh_ends[:, :, :, 1:HALF + 1]
        bc = cut(R_BC, 2, 2, 2, HALF)

        mod_w = cut(R_UH, 2, C, 3 * DM)
        cond_w = cut(R_UH + 3072, 2, C, DM)
        w_up0 = cut(R_W, 2, C, MH0)
        w_down0 = cut(R_W + 2048, MH0 // P, DM)
        g0 = [cut(at, MH0 // P, HALF) for at in (R_DT, R_XS, 34816, 36864)]
        R_PARTS, R_V, R_AW, R_MW = 16384, 22528, 30720, 34816
        qk_w = cut(R_AW, 2, C, DM)
        v_w = cut(R_AW + 1024, C, HG, P)
        proj_w = cut(R_AW + 2048, HG, DM)
        w_up1 = cut(R_MW, C, 2 * MH1)
        w_down1 = cut(R_MW + 4096, MH1 // P, DM)
        qk = cut(R_BC, 2, C, L)
        qk_parts = cut(R_PARTS, 6144).bitcast(BF16).rearrange("p (a w c t) -> p a w c t", a=PARTS, w=2, c=C)
        all_stacks = cut(R_W, STACKS * 4096).bitcast(BF16).rearrange("p (u w j t) -> p u w j t", u=STACKS, w=2, j=4)
        STACK_AT = (1, 0, 2)
        stack = [all_stacks[:, at] for at in STACK_AT]
        v_aug = cut(R_V, B, QT, HG, P)
        attnT = [cut(R_H, HG, L), cut(R_V, HG, L)]
        probs = cut(R_BC, 4, 2, HALF)
        g1 = [cut(R_XS + k * 4096, MH1 // P, HALF) for k in range(2)]
        h1 = cut(R_W, C, B, L)
        NORM_AT = {"ln0": (24064, 28160), "ln1": (26112, 22016), "rms0": (26624, 28672), "rms1": (26624, 28672)}
        sq = {name: cut(at, 2, C, HALF) for name, (at, _) in NORM_AT.items()}
        rstd = {name: cut(at, 4, HALF) for name, (_, at) in NORM_AT.items()}

        mask_i = cut(38912, B, L)[0:1].bitcast(I32)
        mask_f = cut(24064, B, L)[0:1]
        mask_d = cut(38912, B, L)[0:1]
        mask_b = cut(R_MW + 6144, L)[0:1].bitcast(BF16).rearrange("p (b t) -> p b t", b=B)

        bc_rows = sb("bc_rows", [P, HALF])
        attn_sb = sb("attn_sb", [P, 2, HALF])
        a_neg = sb("a_neg", [P, 2, NI, DS])
        carry = sb("carry", [P, 2, DS, NI, 2])
        zero_ends = sb("zero_ends", [P, NI, 2])
        ident = sb("ident", [P, P])
        ones = sb("ones", [P, P])
        mean_w = sb("mean_w", [P, P])
        ident_b = sb("ident_b", [P, P], BF16)
        sum_sel = sb("sum_sel", [P, P])
        any_row = sb("any_row", [1, B])
        q_scale = sb("q_scale", [P, B])
        cond = sb("cond", [P, C, B])
        cond_silu = sb("cond_silu", [P, C, B])
        mod_b = sb("mod_b", [P, 2, 6])
        mods = sb("mods", [P, 2, 6, B])
        cond_b = sb("cond_b", [P, 2, C])
        cmod = sb("cmod", [P, 2, C, B])
        norm_w = sb("norm_w", [P, C])
        dt_bias = sb("dt_bias", [P, 2, NI])
        d_skip = sb("d_skip", [P, 2, NI])
        b_up1 = sb("b_up1", [P, 2 * MH1 // P])
        b_down1 = sb("b_down1", [P, C])
        b_proj = sb("b_proj", [P, C])
        eps = sb("eps", [P, 1])
        row_max = sb("row_max", [P, QT, 4, HALVES])
        top = sb("top", [P, QT, 4])
        top_rest = sb("top_rest", [P, QT, 4])
        top_parts = sb("top_parts", [P, QT, 4, 4], BF16)

        psum = ctx.enter_context(nc.psum_tensor("psum", [P, 8, HALF], F32))
        qk_dram = nc.dram_tensor("qk_dram", [B, PARTS, 2, DM, L], BF16).ap()
        bc_dram = nc.dram_tensor("bc_dram", [UNITS, P, HALF], F32).ap()

        names = """const_ready cond_in mamba_w_in modw_in dt_bias_in mask_in x_in_0 x_in_1 x_in_2 x_in_3
            norm_in ssm_w_in out_w_in ssm_small_in mlp0_in attn_w_in mlp1_in bc_out store_out
            cond_silu_ready mods_ready mods_step mask_step mask_ready any_full q_scale_ready
            tile_full tile_free_act tile_free_dve
            centred squared rstd_ready normed h_ready
            exp_step dt_ready dtx_ready skip_ready bc_rows_ready a_exp a_ready
            ends_ready decay_ready scan_done u_ready prod_done reduce_done sum_ready gated
            x_updated mid_step
            pad_zero scores_full scores_free max_step top_ready rows_full_0 rows_full_1 rows_ready_0 rows_ready_1
            hi_ready rest_ready mid_ready lo_ready qk_out ones_set stack_in_0 stack_in_1 stack_in_2
            s2_full probs_ready pv_done attn_copied sums_full sums_copied recip_ready attn_ready v_ready
            b_in_0 b_in_1 c_in_0 c_in_1""".split()
        s = {n: sem(n) for n in names}

        FREES = {"a": ("tile_free_act", 1), "d": ("tile_free_dve", 1), "x": ("x_updated", 1),
                 "c": ("centred", C), "r": ("bc_rows_ready", 1)}
        eaters, first = [], {}

        def tiles(name, who):
            first[name] = len(eaters)
            eaters.extend(who)

        def unit(u):
            d, r = divmod(u, B * HALVES)
            b, hi = divmod(r, HALVES)
            return d, b, hi, (1 - hi if d else hi)

        NORMS = ("ln0", "ln1", "rms0", "rms1")
        LATE_ORDER = [b * HALVES + half for d, b, _, half in map(unit, range(UNITS // 2, UNITS))]
        ORDER = {"ln0": list(range(CHUNKS)), "ln1": LATE_ORDER, "rms0": LATE_ORDER, "rms1": list(range(CHUNKS))}
        HIDDEN = {"ln1": MH0 // P, "rms1": MH1 // P}

        def up(name, i, m0, m1):
            return [("up", name, i, m) for m in range(m0, m1)]

        def down(name, i):
            return [("down", name, i, c) for c in range(C)]

        def steps(kinds, name, *places):
            return [(kind, name, i) for i in places for kind in kinds.split()]

        N0, N1 = 2 * MH0 // P, 2 * MH1 // P
        START = steps("mean centre square sum std", "ln0", 0) + [("mods", 0)] + steps("scale", "ln0", 0)\
            + [("xs", 0), ("bc", 0)] + [("dt", 0, f) for f in range(NI)]\
            + [("mods", 1), ("mods", 2), ("decay rate",), ("softplus", 0)] + [("zs", 0, f) for f in range(NI)]\
            + steps("mean centre square sum std scale", "ln0", 1)
        BESIDE = [[("out", UNITS - 2)],
                  steps("mean centre", "ln1", 0, 1),
                  steps("mean centre", "ln1", 2) + steps("square", "ln1", 0, 1),
                  steps("sum", "ln1", 0, 1) + steps("square", "ln1", 2),
                  steps("sum", "ln1", 2) + steps("std", "ln1", 0, 1, 2) + steps("scale", "ln1", 0),
                  up("ln1", 0, 0, 2) + steps("scale", "ln1", 1),
                  up("ln1", 0, 2, 4) + steps("scale", "ln1", 2),
                  up("ln1", 0, 4, 6), up("ln1", 0, 6, 8), down("ln1", 0)[:1], down("ln1", 0)[1:],
                  up("ln1", 1, 0, 2), up("ln1", 1, 2, 4), up("ln1", 1, 4, 6), up("ln1", 1, 6, 8)]

        def v_steps(b, t0, t1):
            return [("v", b, kt) for kt in range(t0, t1)]

        def first_pass(w0, w1):
            return [("first pass", w0, w1)]

        QK_TILES = 2 * C * HALVES
        QK_ORDER = list(range(QK_TILES // 2, QK_TILES)) + list(range(QK_TILES // 2))
        LATE = [("out", UNITS - 1)] + down("ln1", 1) + steps("mean centre square", "ln1", 3)\
            + up("ln1", 2, 0, 4) + steps("sum std scale", "ln1", 3) + steps("square", "rms0", 0, 1)\
            + up("ln1", 2, 4, N0) + steps("sum std scale", "rms0", 0, 1) + up("ln1", 3, 0, 4) + [("mask",)]\
            + [("qk", 0, m) for m in QK_ORDER[:4]] + [("any key",)] + [("qk", 0, m) for m in QK_ORDER[4:]]\
            + [("first part", 0), ("rest", 0)] + down("ln1", 2) + [("second part", 0)] + up("ln1", 3, 4, N0)\
            + [("third part", 0)] + steps("square sum std", "rms0", 2) + down("ln1", 3)\
            + steps("scale", "rms0", 2) + steps("square", "rms0", 3) + v_steps(0, 0, 3)\
            + steps("sum std scale", "rms0", 3) + v_steps(0, 3, QT) + [("ones of v", 0)] + first_pass(0, 8)
        for n, m in enumerate(QK_ORDER):
            LATE += [("qk", 1, m)] + first_pass(8 + 4 * n, 12 + 4 * n)
        LATE += [("first part", 1)] + first_pass(40, 42) + [("rest", 1)]
        for m in range(QT):
            LATE += v_steps(1, m, m + 1) + first_pass(42 + 3 * m, 45 + 3 * m)
            if m == 3:
                LATE += [("second part", 1)]
            if m == 6:
                LATE += [("third part", 1)]
        LATE += [("ones of v", 1)] + first_pass(66, SCORE_TILES + LEAD)
        END = [("proj", 0), ("proj", 1)] + steps("square sum std", "rms1", 0) + [("proj", 2)]\
            + steps("scale", "rms1", 0) + steps("square sum std", "rms1", 1) + [("proj", 3)]\
            + up("rms1", 0, 0, 4) + steps("scale", "rms1", 1)\
            + up("rms1", 0, 4, 8) + steps("square sum std scale", "rms1", 2) + up("rms1", 0, 8, 12)\
            + steps("square sum std scale", "rms1", 3) + up("rms1", 0, 12, N1)
        for i in range(1, CHUNKS):
            END += up("rms1", i, 0, N1) + down("rms1", i - 1)
        END += down("rms1", CHUNKS - 1)

        last_update, NEED = {}, {}

        def place_tiles(order):
            for step in order:
                kind, *at = step
                if kind in ("mean", "square") and (at[0], at[1]) not in NEED:
                    NEED[at[0], at[1]] = last_update.get(ORDER[at[0]][at[1]], 0)
                who = {"mods": "d", "mean": "c", "sum": "a", "down": "x", "out": "x" * C, "proj": "x" * C,
                       "xs": "a" * NI, "zs": "a", "dt": "a", "bc": "r",
                       "qk": "a", "v": "a"}.get(kind, "")
                if kind == "up":
                    who = "da"[at[2] % 2 == 0]
                tiles(step, who)
                if kind == "out":
                    d, b, hi, half = unit(at[0])
                    last_update[b * HALVES + half] = eaters.count("x")
                if kind == "down":
                    last_update[ORDER[at[0]][at[1]]] = eaters.count("x")
                if kind == "proj":
                    last_update[at[0]] = eaters.count("x")

        def beside_unit(g, u):
            nxt = [[], [("xs", u + 1)], [("bc", u + 1), ("dt", u + 1, 0)], [("dt", u + 1, 1), ("dt", u + 1, 2)],
                   [("dt", u + 1, 3), ("zs", u + 1, 0), ("zs", u + 1, 1)],
                   [("softplus", u + 1), ("zs", u + 1, 2), ("zs", u + 1, 3)], [], []]
            own = [[("out", u - 1)]] if u else [steps("mean centre", "ln0", 2, 3), steps("square", "ln0", 2, 3),
                                                steps("sum std", "ln0", 2, 3) + steps("scale", "ln0", 2),
                                                steps("scale", "ln0", 3)]
            return (own[g] if g < len(own) else []) + nxt[g]

        place_tiles(START)
        for u in range(UNITS - 1):
            for g in range(SEGS):
                place_tiles(beside_unit(g, u))
        for turn in BESIDE:
            place_tiles(turn)
        place_tiles(LATE)
        place_tiles(END)

        def eaten(g, who):
            return sum(e == who for e in eaters[:g + 1])

        def bank(g):
            return psum[:, 4 + g % 4, :]

        def take(pe, g):
            if g >= 4:
                name, each = FREES[eaters[g - 4]]
                pe.wait_ge(s[name], each * eaten(g - 4, eaters[g - 4]))
            return bank(g)

        SIDE_BANKS = (5, 6, 7, 3)
        ALONE = SCORE_TILES + LEAD
        SIDE_FREES = {"scores": "scores_free", "rows_0": "rows_ready_0", "rows_1": "rows_ready_1",
                      "sums": "sums_copied"}
        side, place = [], {}

        def side_tile(kind, i):
            place[kind, i] = len(side)
            side.append((kind, i))

        BLOCKS = B * HG * HALVES
        ALL_SCORES = B * HG * SCORE_TILES

        def scores_at(v, m):
            w = (v + 2) * SCORE_TILES // 2 + 2 * m + LEAD
            return range(min(w, ALL_SCORES), min(w + 2, ALL_SCORES))

        def rows_at(v, m):
            if m not in ROW_STEPS or (v % 2 and v // 2 + 1 == B * HG):
                return None
            return 1 - v % 2, (v + 1) // 2, ROW_STEPS.index(m)

        for j in range(4):
            side_tile("rows_0", j)
        for v in range(BLOCKS):
            for m in range(BLOCK):
                for w in scores_at(v, m):
                    side_tile("scores", w)
                if m == SUMS_STEP and v:
                    side_tile("sums", v - 1)
                if rows_at(v, m):
                    half, u, j = rows_at(v, m)
                    side_tile(f"rows_{half}", 4 * u + j)
        side_tile("sums", BLOCKS - 1)

        def side_bank(kind, i):
            if kind == "scores" and i < ALONE:
                return psum[:, i % 4, :]
            return psum[:, SIDE_BANKS[place[kind, i] % 4], :]

        def take_side(pe, kind, i):
            if kind == "scores" and i < ALONE:
                if i >= 4:
                    pe.wait_ge(s["scores_free"], i - 3)
                return side_bank(kind, i)
            p = place[kind, i]
            if p >= 4:
                before, n = side[p - 4]
                pe.wait_ge(s[SIDE_FREES[before]], n + 1)
            return side_bank(kind, i)

        def tok(half):
            return slice(half * HALF, (half + 1) * HALF)

        def chunk(name, i):
            return divmod(ORDER[name][i], HALVES)

        block = ctx.enter_context(nc.Block())

        @block.sync
        def _(sp):
            def load(dst, src, name):
                sp.dma_start(dst, src).then_inc(s[name], 16)

            def kp(ap, n):
                return ap.rearrange("(c p) n -> p c n", p=P)

            def unit_weights(d):
                pre = ("fwd_", "bwd_")[d]
                load(in_w, kp(t[pre + "in_w"], 0), "ssm_w_in")
                load(xproj_w, kp(t[pre + "xproj_w"], 0), "ssm_w_in")

            load(cond[:, :, :], kp(t["cond"], B), "cond_in")
            for q in range(CHUNKS):
                b, half = divmod(q, HALVES)
                load(x[:, :, b, tok(half)], kp(t["x"][b, :, tok(half)], 0), f"x_in_{q}")
                if q == 0:
                    load(mod_w[:, 0], kp(t["mamba_w"], 0), "mamba_w_in")
                    load(mod_b[:, 0, :], t["mamba_b"], "mamba_w_in")
                    unit_weights(0)
                    load(dt_bias[:, 0], t["fwd_dt_bias"], "dt_bias_in")
            load(mod_w[:, 1], kp(t["mlp_w"], 0), "modw_in")
            load(mod_b[:, 1, :], t["mlp_b"], "modw_in")
            load(cond_w[:, 0], kp(t["shift_w"], 0), "modw_in")
            load(cond_w[:, 1], kp(t["scale_w"], 0), "modw_in")
            for k, name in enumerate(("shift_b", "scale_b")):
                load(cond_b[:, k, :], t[name], "modw_in")
            load(norm_w[:, :], t["norm_w"], "modw_in")
            load(dt_bias[:, 1], t["bwd_dt_bias"], "ssm_small_in")
            for d, pre in enumerate(("fwd_", "bwd_")):
                load(a_neg[:, d], kp(t[pre + "A_log"], 0), "ssm_small_in")
                load(d_skip[:, d], t[pre + "D"], "ssm_small_in")
            load(b_up1[:, :], t["up1_b"], "norm_in")
            load(b_down1[:, :], t["down1_b"], "norm_in")
            load(b_proj[:, :], t["proj_b"], "norm_in")
            load(out_w, kp(t["fwd_out_w"], 0), "out_w_in")
            for u in range(UNITS):
                d, b, hi, half = unit(u)
                base = u * DS
                sp.wait_ge(s["bc_rows_ready"], u + 1)
                sp.dma_start(bc_dram[u], bc_rows[:, :]).then_inc(s["bc_out"], 16)
                sp.wait_ge(s["bc_out"], 16 * (u + 1))

                def row_pair(pair, k, row):
                    if row == 0:
                        sp.wait_ge(s["u_ready"], pair * 2 + (base + 2))
                    else:
                        sp.wait_ge(s["prod_done"], pair * 2 + (base + 2))
                    src = bc_dram[u, bass.ds(pair * 2 + row * DS, 2), :]
                    sp.dma_start(bc[:, k, row], src.partition_broadcast(P))\
                      .then_inc(s[f"{'bc'[row]}_in_{k}"], 16)

                row_pair(0, 0, 0)
                with sp.Fori(0, DS // 4 - 1) as i:
                    for k in range(2):
                        row_pair(i * 2 + (k + 1), 1 - k, 0)
                        row_pair(i * 2 + k, k, 1)
                row_pair(DS // 2 - 1, 1, 0)
                row_pair(DS // 2 - 2, 0, 1)
                row_pair(DS // 2 - 1, 1, 1)
                if u == UNITS // 2 - 2:
                    sp.wait_ge(s["tile_full"], first["zs", u + 1, NI - 1] + 1)
                    unit_weights(1)
                if u == UNITS // 2:
                    sp.wait_ge(s["tile_full"], first["out", u - 1] + C)
                    load(out_w, kp(t["bwd_out_w"], 0), "out_w_in")
                if u == UNITS - 2:
                    sp.wait_ge(s["tile_full"], first["zs", u + 1, NI - 1] + 1)
                    for k, name in enumerate(("mlp_w1", "mlp_w2")):
                        load(w_up0[:, k], kp(t[name], 0), "mlp0_in")
                    load(w_down0, kp(t["mlp_w3"], 0), "mlp0_in")
            sp.wait_ge(s["pad_zero"], 1)
            load(mask_i[:, :, :], t["mask"].rearrange("(a b) n -> a b n", a=1), "mask_in")
            for k in range(2):
                load(qk_w[:, k], kp(t["qkv_w"][:, k * DM:(k + 1) * DM], 0), "attn_w_in")
            for c in range(C):
                src = t["qkv_w"][c * P:(c + 1) * P, 2 * DM:3 * DM]
                dst = v_w[:, c].rearrange("p g (j e) -> p (g j) e", e=HP)[:, :, 0:HD]
                load(dst, src.rearrange("p (h e) -> p h e", e=HD), "attn_w_in")
            pr = t["proj_w"].rearrange("(g j e) n -> j e g n", j=4, e=HD)
            for j in range(4):
                load(proj_w[32 * j:32 * j + HD], pr[j], "attn_w_in")
            def store_parts(b):
                sp.wait_ge(s["lo_ready"], b + 1)
                for a in range(PARTS):
                    for w in range(2):
                        sp.dma_start(qk_dram[b, a, w].rearrange("(c p) t -> p c t", p=P), qk_parts[:, a, w])\
                          .then_inc(s["qk_out"], 16)

            store_parts(0)
            for u in range(B * HG):
                b, hg = divmod(u, HG)
                if u == 1:
                    sp.wait_ge(s["x_updated"], eaten(first["down", "ln1", CHUNKS - 1, C - 1], "x"))
                    load(w_up1, kp(t["up1_w"], 0), "mlp1_in")
                    load(w_down1, kp(t["down1_w"], 0), "mlp1_in")
                if u == 2:
                    store_parts(1)
                if u in (0, 2):
                    sp.wait_ge(s["qk_out"], 16 * 2 * PARTS * (u // 2 + 1))
                if u < STACKS:
                    sp.wait_ge(s["ones_set"], u + 1)
                if u >= STACKS:
                    sp.wait_ge(s["s2_full"], (u - STACKS + 1) * 4 * BLOCK)
                for w, parts in enumerate((Q_PARTS, K_PARTS)):
                    for r, a in enumerate(parts):
                        rows = qk_dram[b, a, w, hg * 4 * HD:(hg + 1) * 4 * HD, :]
                        sp.dma_start(stack[u % STACKS][r * HD:(r + 1) * HD, w], rows.rearrange("(j e) t -> e j t", e=HD))\
                          .then_inc(s[f"stack_in_{u % STACKS}"], 16)
                sp.dma_start(stack[u % STACKS][ONE_ROW:ONE_ROW + 1, 1],
                             mask_b[:, b:b + 1, :].to_broadcast([1, 4, L])).then_inc(s[f"stack_in_{u % STACKS}"], 16)
            for q in range(CHUNKS):
                b, half = chunk("rms1", q)
                sp.wait_ge(s["x_updated"], eaten(first["down", "rms1", q, C - 1], "x"))
                for c in range(C):
                    sp.dma_start(t["out"][b, c * P:(c + 1) * P, tok(half)], x[:, c, b, tok(half)])\
                      .then_inc(s["store_out"], 16)
            sp.wait_ge(s["store_out"], 16 * CHUNKS * C)

        @block.gpsimd
        def _(pool):
            pool.memset(ident[:, :], 0.0).then_inc(s["const_ready"], 1)
            pool.memset(sum_sel[:, :], 0.0).then_inc(s["const_ready"], 1)
            pool.memset(ones[:, :], 1.0).then_inc(s["const_ready"], 1)
            pool.memset(mean_w[:, :], 1.0 / DM).then_inc(s["const_ready"], 1)
            pool.memset(ident_b[:, :], 0.0).then_inc(s["const_ready"], 1)
            pool.memset(top_parts[:, :, :, :], 1.0).then_inc(s["const_ready"], 1)
            pool.memset(eps[:, :], 1e-5).then_inc(s["const_ready"], 1)
            pool.wait_ge(s["const_ready"], 7)
            pool.affine_select(out=ident[:, :], in_=ident[:, :], compare_op=ALU.not_equal, fill=1.0,
                               base=0, pattern=[[-1, P]], channel_multiplier=1).then_inc(s["const_ready"], 1)
            sel = sum_sel[:, :].rearrange("p (j e) -> p j e", e=HP)
            pool.affine_select(out=sel, in_=sel, compare_op=ALU.not_equal, fill=1.0, base=-HD,
                               pattern=[[-HP, 4], [0, HP]], channel_multiplier=1).then_inc(s["const_ready"], 1)
            pool.affine_select(out=ident_b[:, :], in_=ident_b[:, :], compare_op=ALU.not_equal, fill=1.0,
                               base=0, pattern=[[-1, P]], channel_multiplier=1).then_inc(s["const_ready"], 1)

            for u in range(UNITS):
                base = u * DS
                pool.wait_ge(s["dt_ready"], u + 1)
                pool.tensor_tensor(dtx[:, u % 2], dt_[:, u % 2], xs[:, u % 2], ALU.mult).then_inc(s["dtx_ready"], 1)
                pool.wait_ge(s["dtx_ready"], u + 1)
                with pool.Fori(0, DS // 4) as i:
                    for k in range(4):
                        if k % 2 == 0:
                            pool.wait_ge(s[f"b_in_{k // 2}"], i * 16 + (base // 4 + 1) * 16)
                        pool.wait_ge(s["reduce_done"], i * 4 + (base + k + 1))
                        b_row = bc[:, k // 2, 0, k % 2].unsqueeze(1).to_broadcast([P, NI, HALF])
                        pool.tensor_tensor(uh[:, k], dtx[:, u % 2], b_row, ALU.mult).then_inc(s["u_ready"], 1)
            pool.wait_ge(s["reduce_done"], SCAN_TILES + 4)
            pool.memset(arena[:, R_AW + 1024:R_AW + 4096], 0.0).then_inc(s["pad_zero"], 1)
            pool.wait_ge(s["pad_zero"], 1)
            for at, name, count in ((STACK_AT[0], "x_updated", eaten(first["down", "ln1", 1, C - 1], "x")),
                                    (STACK_AT[1], "x_updated", eaten(first["down", "ln1", CHUNKS - 1, C - 1], "x")),
                                    (STACK_AT[2], "qk_out", 16 * 2 * PARTS * B)):
                pool.wait_ge(s[name], count)
                if at != STACK_AT[0]:
                    pool.wait_ge(s["ones_set"], STACK_AT.index(at))
                pool.memset(arena[ONE_ROW:ROWS, R_W + at * 4096:R_W + (at + 1) * 4096], TWO_ONES)\
                    .then_inc(s["ones_set"], 1)
            for v in range(BLOCKS):
                u, qh = divmod(v, HALVES)
                b, hg = divmod(u, HG)
                pool.wait_ge(s["recip_ready"], 4 * (v + 1))
                pool.tensor_tensor(attnT[b][:, hg, tok(qh)], attn_sb[:, 0], attn_sb[:, 1], ALU.mult)\
                    .then_inc(s["attn_ready"], 1)

        @block.scalar
        def _(act):
            def square(name, i):
                b, half = chunk(name, i)
                n = CHUNKS * NORMS.index(name) + i
                if name.startswith("ln"):
                    act.wait_ge(s["centred"], (n + 1) * C)
                else:
                    act.wait_ge(s["x_updated"], NEED[name, i])
                if i >= 2:
                    act.wait_ge(s["tile_full"], first["sum", name, i - 2] + 1)
                src = (h if name.startswith("ln") else x)[:, :, b, tok(half)]
                act.activation(sq[name][:, i % 2], src, ACT.Square).then_inc(s["squared"], 1)

            def std(name, i):
                g = first["sum", name, i]
                act.wait_ge(s["tile_full"], g + 1)
                act.activation(rstd[name][:, i], bank(g), ACT.Sqrt,
                               bias=(eps[:, 0:1] if name.startswith("ln") else 0.0))\
                   .then_inc(s["tile_free_act"], 1)

            act.wait_ge(s["cond_in"], 16)
            act.activation(cond_silu[:, :, :], cond[:, :, :], ACT.Silu).then_inc(s["cond_silu_ready"], 1)
            act.wait_ge(s["const_ready"], 10)

            def silu_path(out, g):
                act.wait_ge(s["tile_full"], g + 1)
                act.activation(out, bank(g), ACT.Silu).then_inc(s["tile_free_act"], 1)

            def raw_dt(u, f):
                g = first["dt", u, f]
                if u == 0 and f == 0:
                    act.wait_ge(s["dt_bias_in"], 16)
                if u == 1 and f == 0:
                    act.wait_ge(s["ssm_small_in"], 80)
                act.wait_ge(s["tile_full"], g + 1)
                act.activation(dt_[:, u % 2, f], bank(g), ACT.Identity, bias=dt_bias[:, unit(u)[0], f:f + 1])\
                   .then_inc(s["tile_free_act"], 1)
                if f == NI - 1:
                    abs_dt(u)

            def abs_dt(u):
                act.wait_ge(s["tile_free_act"], eaten(first["dt", u, NI - 1], "a"))
                act.activation(dtx[:, u % 2], dt_[:, u % 2], ACT.Abs).then_inc(s["exp_step"], 1)

            def log_dt(u):
                act.wait_ge(s["exp_step"], 3 * u + 1)
                act.activation(dtx[:, u % 2], dtx[:, u % 2], ACT.Exp, scale=-1.0).then_inc(s["exp_step"], 1)
                act.wait_ge(s["exp_step"], 3 * u + 2)
                act.activation(dtx[:, u % 2], dtx[:, u % 2], ACT.Ln, bias=1.0).then_inc(s["exp_step"], 1)

            def skip(u):
                act.wait_ge(s["dtx_ready"], u + 1)
                for f in range(NI):
                    act.activation(xs[:, u % 2, f], xs[:, u % 2, f], ACT.Copy,
                                   scale=d_skip[:, unit(u)[0], f:f + 1]).then_inc(s["skip_ready"], 1)

            def do(order):
                for kind, *at in order:
                    if kind == "square":
                        square(*at)
                    if kind == "std":
                        std(*at)
                    if kind == "xs":
                        for f in range(NI):
                            silu_path(xs[:, at[0] % 2, f], first["xs", at[0]] + f)
                    if kind == "zs":
                        u, f = at
                        silu_path(zs[:, u % 2, f], first["zs", u, f])
                    if kind == "dt":
                        raw_dt(*at)
                    if kind == "softplus":
                        log_dt(*at)
                    if kind == "decay rate":
                        act.wait_ge(s["ssm_small_in"], 80)
                        act.activation(a_neg[:, :, :, :], a_neg[:, :, :, :], ACT.Exp).then_inc(s["a_exp"], 1)
                    if kind == "up":
                        silu_up(*at)
                    if kind == "qk":
                        copy_qk(*at)
                    if kind == "v":
                        copy_v(*at)
                    if kind == "any key":
                        softmax_scale()
                    if kind == "first part":
                        first_part(*at)
                    if kind == "second part":
                        act.wait_ge(s["rest_ready"], at[0] + 1)
                        act.activation(qk_parts[:, 1], qk, ACT.Copy).then_inc(s["mid_ready"], 1)

            def silu_up(name, i, m):
                if m % 2:
                    return
                if name == "rms1" and m == 0 and i >= 2:
                    act.wait_ge(s["tile_full"], first["down", name, i - 2, C - 1] + 1)
                g = first["up", name, i, m]
                out = (g0[i] if name == "ln1" else g1[i % 2])[:, m // 2]
                act.wait_ge(s["tile_full"], g + 1)
                act.activation(out, bank(g), ACT.Silu,
                               bias=(b_up1[:, m // 2:m // 2 + 1] if name == "rms1" else 0.0))\
                   .then_inc(s["tile_free_act"], 1)

            def softmax_scale():
                act.wait_ge(s["any_full"], 1)
                act.activation(q_scale[:, :], psum[:, 0, 0:B], ACT.Copy, scale=HD ** -0.5)\
                   .then_inc(s["q_scale_ready"], 1)
                act.wait_ge(s["q_scale_ready"], 1)

            def copy_qk(b, m):
                if b and m == QK_ORDER[0]:
                    act.wait_ge(s["lo_ready"], b)
                g = first["qk", b, m]
                w, r = divmod(m, C * HALVES)
                c, half = divmod(r, HALVES)
                act.wait_ge(s["tile_full"], g + 1)
                act.activation(qk[:, w, c, tok(half)], bank(g), ACT.Copy,
                               scale=(1.0 if w else q_scale[:, b:b + 1])).then_inc(s["tile_free_act"], 1)

            def first_part(b):
                act.wait_ge(s["tile_free_act"], eaten(first["qk", b, QK_ORDER[-1]], "a"))
                if b:
                    act.wait_ge(s["qk_out"], 16 * 2 * PARTS * b)
                act.activation(qk_parts[:, 0], qk, ACT.Copy).then_inc(s["hi_ready"], 1)

            def copy_v(b, kt):
                g = first["v", b, kt]
                act.wait_ge(s["tile_full"], g + 1)
                act.activation(v_aug[:, b, kt].rearrange("p g e -> p (g e)"), bank(g), ACT.Copy)\
                   .then_inc(s["tile_free_act"], 1)

            do(START)
            act.wait_ge(s["a_ready"], 1)
            ones_ends = ones[:, 0:2 * NI].rearrange("p (a f) -> p a f", f=NI)
            for u in range(UNITS):
                d, b, hi, half = unit(u)
                base = u * DS
                skip(u)

                enter, leave = (HALF + 1, 0) if d else (0, HALF + 1)

                def save(st, k):
                    act.activation(carry[:, d, bass.ds(st, 1), :, d].rearrange("p a b -> p (a b)"),
                                   uh_ends[:, k, :, leave], ACT.Copy)

                def decays(st, k, saves):
                    act.wait_ge(s["scan_done"], st + (base + 1))
                    if saves:
                        save(st - 2, (k + 2) % 4)
                    ends = carry[:, d, bass.ds(st, 1)].rearrange("p a f e -> p (a f) e") if hi else zero_ends[:, :, :]
                    act.activation(uh_ends[:, k, :, 0:HALF + 2:HALF + 1], ends, ACT.Copy)
                    for f in range(NI):
                        e = act.activation(decay[:, k % 2, f], dt_[:, u % 2, f], ACT.Exp,
                                           scale=a_neg[:, d, f, bass.ds(st, 1)])
                    e.then_inc(s["decay_ready"], 1)

                if hi == 0 and b == 0:
                    act.wait_ge(s["scan_done"], base + 2)
                    for at, value in ((enter, 0.0), (leave, 1.0)):
                        act.activation(decay_ends[:, :, :, at], ones_ends, ACT.Copy, scale=value)\
                           .then_inc(s["ends_ready"], 1)
                if u == UNITS - 1:
                    for g in range(DS // 4):
                        for k in range(4):
                            decays(g * 4 + k, k, False)
                        if g:
                            do(BESIDE[g - 1])
                    continue
                for g in range(SEGS):
                    if g == 0:
                        for st in range(4 * ITERS):
                            decays(st, st % 4, hi == 0 and st >= 2)
                    else:
                        with act.Fori(g * ITERS, (g + 1) * ITERS) as i:
                            for k in range(4):
                                decays(i * 4 + k, k, hi == 0)
                        do(beside_unit(g - 1, u))
                if hi == 0:
                    act.wait_ge(s["scan_done"], base + DS + 2)
                    save(DS - 2, 2)
                    save(DS - 1, 3)

            do(LATE)

            def copy_attn(v):
                act.wait_ge(s["pv_done"], (v + 1) * QT)
                if v:
                    act.wait_ge(s["attn_ready"], v)
                act.activation(attn_sb[:, 0], psum[:, 4], ACT.Copy).then_inc(s["attn_copied"], 1)

            def copy_sums(v):
                act.wait_ge(s["sums_full"], v + 1)
                act.activation(attn_sb[:, 1], side_bank("sums", v), ACT.Copy).then_inc(s["sums_copied"], 1)

            def copy_max_rows(half, u, j):
                act.wait_ge(s[f"rows_full_{half}"], u * 4 + j + 1)
                act.activation(stack[u % STACKS][ONE_ROW:ROWS, 0, j, tok(half)],
                               side_bank(f"rows_{half}", 4 * u + j)[ONE_ROW:ROWS], ACT.Copy)\
                   .then_inc(s[f"rows_ready_{half}"], 1)

            for j in range(4):
                copy_max_rows(0, 0, j)
            for v in range(BLOCKS):
                for m in range(BLOCK):
                    w = v * BLOCK + m
                    if w >= 4:
                        act.wait_ge(s["pv_done"], w // 2 - 1)
                    for jj in range(2):
                        n = 2 * w + jj
                        act.wait_ge(s["s2_full"], n + 1)
                        act.activation(probs[:, w % 4, jj], psum[:, n % 3, :], ACT.Exp)\
                           .then_inc(s["probs_ready"], 1)
                    if m == 2 and v:
                        copy_attn(v - 1)
                    if m == SUMS_STEP and v:
                        copy_sums(v - 1)
                    if rows_at(v, m):
                        copy_max_rows(*rows_at(v, m))
            copy_attn(BLOCKS - 1)
            copy_sums(BLOCKS - 1)
            do(END)

        @block.vector
        def _(dve):
            dve.memset(carry[:, :, :, :, :], 0.0).then_inc(s["reduce_done"], 4)
            dve.memset(zero_ends[:, :, :], 0.0)
            dve.memset(top[:, :, :], 0.0).then_inc(s["scan_done"], 2)
            dve.memset(row_max[:, :, :, :], 0.0).then_inc(s["prod_done"], 4)
            dve.memset(attn_sb[:, :, :], 0.0).then_inc(s["u_ready"], 4)

            def modulation(part):
                g = first["mods", part]
                dve.wait_ge(s["tile_full"], g + 1)
                if part < 2:
                    dve.wait_ge(s["modw_in" if part else "mamba_w_in"], 112 if part else 32)
                    dve.tensor_tensor(mods[:, part], bank(g)[:, 0:6 * B].rearrange("p (a b) -> p a b", b=B),
                                      mod_b[:, part, :].unsqueeze(2).to_broadcast([P, 6, B]), ALU.add)\
                       .then_inc(s["tile_free_dve"], 1)
                    dve.wait_ge(s["tile_free_dve"], part + 1)
                    dve.tensor_scalar(mods[:, part, C:2 * C, :], mods[:, part, C:2 * C, :], 1.0, None, ALU.add)\
                       .then_inc(s["mods_ready"], 1)
                    dve.wait_ge(s["mods_ready"], part + 1)
                    return
                dve.tensor_tensor(cmod[:, :, :, :], bank(g)[:, 0:2 * C * B].rearrange("p (k c b) -> p k c b", k=2, b=B),
                                  cond_b[:, :, :].unsqueeze(3).to_broadcast([P, 2, C, B]), ALU.add)\
                   .then_inc(s["tile_free_dve"], 1)
                dve.wait_ge(s["tile_free_dve"], 3)
                dve.tensor_scalar(cmod[:, 1], cmod[:, 1], 1.0, 0.1, ALU.add, ALU.max).then_inc(s["mods_step"], 1)
                dve.wait_ge(s["mods_step"], 1)
                dve.scalar_tensor_tensor(cmod[:, 1], cmod[:, 1], 10.0,
                                         norm_w[:, :].unsqueeze(2).to_broadcast([P, C, B]), ALU.min, ALU.mult)\
                   .then_inc(s["mods_ready"], 1)
                dve.wait_ge(s["mods_ready"], 3)

            def centre(name, i):
                b, half = chunk(name, i)
                g = first["mean", name, i]
                dve.wait_ge(s["tile_full"], g + 1)
                for c in range(C):
                    dve.tensor_tensor(h[:, c, b, tok(half)], x[:, c, b, tok(half)], bank(g), ALU.subtract)\
                       .then_inc(s["centred"], 1)

            def scale(name, i):
                k = NORMS.index(name)
                n = CHUNKS * k + i
                b, half = chunk(name, i)
                r = rstd[name][:, i]
                centred = name.startswith("ln")
                dve.wait_ge(s["tile_free_act"], eaten(first["sum", name, i], "a"))
                if not centred:
                    dve.wait_ge(s["x_updated"], NEED[name, i])
                    dve.tensor_scalar(r, r, 1e-6, None, ALU.max).then_inc(s["mid_step"], 1)
                    dve.wait_ge(s["mid_step"], n - 2 * CHUNKS + 1)
                dve.reciprocal(r, r).then_inc(s["rstd_ready"], 1)
                dve.wait_ge(s["rstd_ready"], n + 1)
                out = (h1 if name == "rms1" else h)[:, :, b, tok(half)]
                src = out if centred else x[:, :, b, tok(half)]
                dve.tensor_tensor(out, src, r.unsqueeze(1).to_broadcast([P, C, HALF]), ALU.mult)\
                   .then_inc(s["normed"], 1)
                dve.wait_ge(s["normed"], n + 1)
                for c in range(C):
                    if centred:
                        mul, add = mods[:, k, C + c, b:b + 1], mods[:, k, c, b:b + 1]
                    else:
                        mul, add = cmod[:, 1, c, b:b + 1], cmod[:, 0, c, b:b + 1]
                    dve.tensor_scalar(out[:, c], out[:, c], mul, add, ALU.mult, ALU.add).then_inc(s["h_ready"], 1)

            def copy_rows(u):
                g = first["bc", u]
                dve.wait_ge(s["tile_full"], g + 1)
                if u:
                    dve.wait_ge(s["bc_out"], 16 * u)
                dve.tensor_copy(bc_rows[:, :], bank(g)).then_inc(s["bc_rows_ready"], 1)

            def finish_dt(u):
                dve.wait_ge(s["exp_step"], 3 * u + 3)
                dve.scalar_tensor_tensor(dt_[:, u % 2], dt_[:, u % 2], 0.0, dtx[:, u % 2], ALU.max, ALU.add)\
                   .then_inc(s["dt_ready"], 1)

            def add_output(u):
                d, b, hi, half = unit(u)
                for c in range(C):
                    g = first["out", u] + c
                    xc = x[:, c, b, tok(half)]
                    dve.wait_ge(s["tile_full"], g + 1)
                    if u * C + c >= UNITS * C // 2:
                        dve.wait_ge(s["x_updated"], UNITS * C // 2)
                    dve.scalar_tensor_tensor(xc, bank(g), mods[:, 0, 2 * C + c, b:b + 1], xc, ALU.mult, ALU.add)\
                       .then_inc(s["x_updated"], 1)

            def gate(name, i, m):
                if m % 2 == 0:
                    return
                g = first["up", name, i, m]
                gm = (g0[i] if name == "ln1" else g1[i % 2])[:, m // 2]
                dve.wait_ge(s["tile_full"], g + 1)
                dve.wait_ge(s["tile_free_act"], eaten(first["up", name, i, m - 1], "a"))
                at = MH1 // P + m // 2
                add = b_up1[:, at:at + 1] if name == "rms1" else 0.0
                dve.scalar_tensor_tensor(gm, bank(g), add, gm, ALU.add, ALU.mult).then_inc(s["tile_free_dve"], 1)

            def update(name, i, c):
                b, half = chunk(name, i)
                g = first["down", name, i, c]
                xc = x[:, c, b, tok(half)]
                dve.wait_ge(s["tile_full"], g + 1)
                if name == "ln1":
                    o = dve.scalar_tensor_tensor(xc, bank(g), mods[:, 1, 2 * C + c, b:b + 1], xc, ALU.mult, ALU.add)
                else:
                    o = dve.scalar_tensor_tensor(xc, bank(g), b_down1[:, c:c + 1], xc, ALU.add, ALU.add)
                o.then_inc(s["x_updated"], 1)

            def add_attention(q):
                b, half = divmod(q, HALVES)
                for c in range(C):
                    g = first["proj", q] + c
                    xc = x[:, c, b, tok(half)]
                    dve.wait_ge(s["tile_full"], g + 1)
                    dve.scalar_tensor_tensor(xc, bank(g), b_proj[:, c:c + 1], xc, ALU.add, ALU.add)\
                       .then_inc(s["x_updated"], 1)

            def do(order):
                for kind, *at in order:
                    if kind == "mods":
                        modulation(*at)
                    if kind == "centre":
                        centre(*at)
                    if kind == "scale":
                        scale(*at)
                    if kind == "bc":
                        copy_rows(*at)
                    if kind == "softplus":
                        finish_dt(*at)
                    if kind == "decay rate":
                        negate_a()
                    if kind == "out":
                        add_output(*at)
                    if kind == "up":
                        gate(*at)
                    if kind == "down":
                        update(*at)
                    if kind == "mask":
                        key_mask()
                    if kind == "rest":
                        rest(*at)
                    if kind == "third part":
                        third_part(*at)
                    if kind == "ones of v":
                        ones_of_v(*at)
                    if kind == "first pass":
                        for w in range(*at):
                            score_max(w)
                            if w == SCORE_TILES - 1:
                                finish_max(0)
                    if kind == "proj":
                        add_attention(*at)

            def negate_a():
                dve.wait_ge(s["a_exp"], 1)
                dve.tensor_scalar(a_neg[:, :, :, :], a_neg[:, :, :, :], -1.0, None, ALU.mult)\
                   .then_inc(s["a_ready"], 1)

            do(START)
            for u in range(UNITS):
                d, b, hi, half = unit(u)
                base = u * DS

                def along(ap):
                    flat = ap.rearrange("p f t -> p (f t)")
                    return flat[:, ::-1] if d else flat

                def scan(st, k):
                    dve.wait_ge(s["decay_ready"], st + (base + 1))
                    dve.wait_ge(s["u_ready"], st + (base + 5))
                    dve.tensor_tensor_scan(along(uh_ends[:, k]), along(decay_ends[:, k % 2]),
                                           along(uh_ends[:, k]), 0.0, op0=ALU.mult, op1=ALU.add)\
                       .then_inc(s["scan_done"], 1)

                def weigh(st, k):
                    dve.wait_ge(s["scan_done"], st + (base + 3))
                    if k % 2 == 0:
                        dve.wait_ge(s[f"c_in_{k // 2}"], (base // 4 + 1) * 16 + (st - k) * 4)
                    c_row = bc[:, k // 2, 1, k % 2].unsqueeze(1).to_broadcast([P, NI, HALF])
                    dve.tensor_tensor(uh[:, k], uh[:, k], c_row, ALU.mult).then_inc(s["prod_done"], 1)

                if u == UNITS - 1:
                    for g in range(DS // 4):
                        for k in range(4):
                            scan(g * 4 + k, k)
                            weigh(g * 4 + k, k)
                        if g:
                            do(BESIDE[g - 1])
                else:
                    for g in range(SEGS):
                        with dve.Fori(g * ITERS, (g + 1) * ITERS) as i:
                            for k in range(4):
                                scan(i * 4 + k, k)
                                weigh(i * 4 + k, k)
                        if g:
                            do(beside_unit(g - 1, u))
                for f in range(NI):
                    if f < NI - 1:
                        dve.wait_ge(s["sum_ready"], (NI - 1) * u + f + 1)
                    else:
                        dve.wait_ge(s["reduce_done"], base + DS + 4)
                    dve.tensor_tensor(zs[:, u % 2, f], psum[:, f, :], zs[:, u % 2, f], ALU.mult)\
                       .then_inc(s["gated"], 1)

            def key_mask():
                dve.wait_ge(s["mask_in"], 16)
                dve.tensor_scalar(mask_f[:, :, :], mask_i[:, :, :], 0.0, None, ALU.not_equal)\
                   .then_inc(s["mask_step"], 1)
                dve.wait_ge(s["mask_step"], 1)
                dve.tensor_reduce(any_row[:, :], mask_f[:, :, :], axis=AX.X, op=ALU.max).then_inc(s["mask_step"], 1)
                dve.tensor_scalar(mask_d[:, :, :], mask_f[:, :, :], -1.0, BIG, ALU.add, ALU.mult)\
                   .then_inc(s["mask_step"], 1)
                dve.wait_ge(s["mask_step"], 3)
                for b in range(B):
                    dve.tensor_scalar(mask_b[:, b, :], mask_d[:, b, :], any_row[:, b:b + 1], None, ALU.mult)\
                       .then_inc(s["mask_ready"], 1)

            def rest(b):
                dve.wait_ge(s["hi_ready"], b + 1)
                dve.tensor_tensor(qk, qk, qk_parts[:, 0], ALU.subtract).then_inc(s["rest_ready"], 1)

            def third_part(b):
                dve.wait_ge(s["mid_ready"], b + 1)
                dve.tensor_tensor(qk_parts[:, 2], qk, qk_parts[:, 1], ALU.subtract).then_inc(s["lo_ready"], 1)

            def ones_of_v(b):
                dve.wait_ge(s["tile_free_act"], eaten(first["v", b, QT - 1], "a"))
                dve.memset(v_aug[:, b].rearrange("p t g (j e) -> p t (g j) e", e=HP)[:, :, :, HD:HD + 1], 1.0)\
                   .then_inc(s["v_ready"], 1)

            def score_max(w):
                u, m = divmod(w, 4 * QT * HALVES)
                j, r = divmod(m, QT * HALVES)
                qt, kh = divmod(r, HALVES)
                dve.wait_ge(s["scores_full"], w + 1)
                if m == 0 and u:
                    dve.wait_ge(s["top_ready"], 4 * u)
                dve.tensor_reduce(row_max[:, qt, j, kh:kh + 1], side_bank("scores", w), axis=AX.X, op=ALU.max)\
                   .then_inc(s["scores_free"], 1)

            def finish_max(u):
                dve.wait_ge(s["scores_free"], (u + 1) * 4 * QT * HALVES)
                if u:
                    dve.wait_ge(s["rows_full_0"], u * 4)
                    dve.wait_ge(s["rows_full_1"], u * 4)
                dve.tensor_reduce(top[:, :, :], row_max[:, :, :, :], axis=AX.X, op=ALU.max).then_inc(s["top_ready"], 1)
                dve.wait_ge(s["top_ready"], 4 * u + 1)
                dve.tensor_scalar(top_parts[:, :, :, 1], top[:, :, :], -1.0, None, ALU.mult)\
                   .then_inc(s["top_ready"], 1)
                dve.wait_ge(s["top_ready"], 4 * u + 2)
                dve.scalar_tensor_tensor(top_rest[:, :, :], top[:, :, :], -1.0, top_parts[:, :, :, 1],
                                         ALU.mult, ALU.subtract).then_inc(s["max_step"], 1)
                dve.wait_ge(s["max_step"], u + 1)
                dve.tensor_copy(top_parts[:, :, :, 2], top_rest[:, :, :]).then_inc(s["top_ready"], 1)
                dve.wait_ge(s["top_ready"], 4 * u + 3)
                dve.tensor_tensor(top_parts[:, :, :, 3], top_rest[:, :, :], top_parts[:, :, :, 2], ALU.subtract)\
                   .then_inc(s["top_ready"], 1)

            def reciprocals(v, k):
                dve.wait_ge(s["sums_copied"], v + 1)
                part = attn_sb[:, 1, k * HALF // 4:(k + 1) * HALF // 4]
                dve.reciprocal(part, part).then_inc(s["recip_ready"], 1)

            do(LATE)
            for v in range(BLOCKS):
                for m in range(BLOCK):
                    for w in scores_at(v, m):
                        score_max(w)
                        if w % SCORE_TILES == SCORE_TILES - 1:
                            finish_max(w // SCORE_TILES)
                    if m in RECIP_STEPS and v:
                        reciprocals(v - 1, RECIP_STEPS.index(m))
            for k in range(4):
                reciprocals(BLOCKS - 1, k)
            do(END)

        @block.tensor
        def _(pe):
            def product(dst, pairs, last=None):
                for k, (lhsT, rhs) in enumerate(pairs):
                    o = pe.matmul(dst, lhsT, rhs, start=k == 0, stop=k == len(pairs) - 1)
                return o

            def mean(name, i):
                b, half = chunk(name, i)
                if NEED[name, i]:
                    pe.wait_ge(s["x_updated"], NEED[name, i])
                else:
                    pe.wait_ge(s[f"x_in_{i}"], 16)
                dst = take(pe, first["mean", name, i])
                product(dst, [(mean_w[:, :], x[:, c, b, tok(half)]) for c in range(C)]).then_inc(s["tile_full"], 1)

            def mean_square(name, i):
                pe.wait_ge(s["squared"], CHUNKS * NORMS.index(name) + i + 1)
                dst = take(pe, first["sum", name, i])
                product(dst, [(mean_w[:, :], sq[name][:, i % 2, c]) for c in range(C)]).then_inc(s["tile_full"], 1)

            def h_ready(name, i):
                pe.wait_ge(s["h_ready"], C * (CHUNKS * NORMS.index(name) + i + 1))

            def modulation(part):
                dst = take(pe, first["mods", part])
                if part < 2:
                    pe.wait_ge(s["cond_in"], 16)
                    pe.wait_ge(s["modw_in" if part else "mamba_w_in"], 112 if part else 32)
                    for m in range(6):
                        o = product(dst[:, m * B:(m + 1) * B],
                                    [(mod_w[:, part, c, m * P:(m + 1) * P], cond[:, c, :]) for c in range(C)])
                else:
                    pe.wait_ge(s["cond_silu_ready"], 1)
                    for k in range(2):
                        for m in range(C):
                            r = (k * C + m) * B
                            o = product(dst[:, r:r + B],
                                        [(cond_w[:, k, c, m * P:(m + 1) * P], cond_silu[:, c, :]) for c in range(C)])
                o.then_inc(s["tile_full"], 1)

            def in_path(name, u, f, g):
                d, b, hi, half = unit(u)
                pe.wait_ge(s["ssm_w_in"], 32 * (d + 1))
                h_ready("ln0", b * HALVES + half)
                at = (DI if name == "zs" else 0) + f * P
                product(take(pe, g), [(in_w[:, c, at:at + P], h[:, c, b, tok(half)]) for c in range(C)])\
                    .then_inc(s["tile_full"], 1)

            def x_proj(u, f, g):
                pe.wait_ge(s["tile_free_act"], eaten(first["xs", u] + NI - 1, "a"))
                product(take(pe, g), [(xproj_w[:, c, f * P:(f + 1) * P], xs[:, u % 2, c]) for c in range(NI)])\
                    .then_inc(s["tile_full"], 1)

            def out_proj(u):
                d, b, hi, half = unit(u)
                pe.wait_ge(s["out_w_in"], 16 * (d + 1))
                pe.wait_ge(s["gated"], NI * (u + 1))
                for c in range(C):
                    dst = take(pe, first["out", u] + c)
                    product(dst, [(out_w[:, f, c * P:(c + 1) * P], zs[:, u % 2, f]) for f in range(NI)])\
                        .then_inc(s["tile_full"], 1)

            def up_tile(name, i, m):
                b, half = chunk(name, i)
                hidden, which = divmod(m, 2)
                if m == 0:
                    h_ready(name, i)
                    if name == "ln1":
                        pe.wait_ge(s["mlp0_in"], 48)
                    else:
                        pe.wait_ge(s["mlp1_in"], 32)
                        pe.wait_ge(s["norm_in"], 48)
                if name == "ln1":
                    pairs = [(w_up0[:, which, c, hidden * P:(hidden + 1) * P], h[:, c, b, tok(half)]) for c in range(C)]
                else:
                    at = which * MH1 + hidden * P
                    pairs = [(w_up1[:, c, at:at + P], h1[:, c, b, tok(half)]) for c in range(C)]
                product(take(pe, first["up", name, i, m]), pairs).then_inc(s["tile_full"], 1)

            def down_tile(name, i, c):
                n = HIDDEN[name]
                w, gbuf = (w_down0, g0[i]) if name == "ln1" else (w_down1, g1[i % 2])
                pe.wait_ge(s["tile_free_dve"], eaten(first["up", name, i, 2 * n - 1], "d"))
                product(take(pe, first["down", name, i, c]),
                        [(w[:, m, c * P:(c + 1) * P], gbuf[:, m]) for m in range(n)])\
                    .then_inc(s["tile_full"], 1)

            def any_key():
                pe.wait_ge(s["mask_ready"], B)
                pe.matmul(psum[:, 0, 0:B], ones[0:1, :], any_row[:, :], start=True, stop=True)\
                  .then_inc(s["any_full"], 1)

            def qk_tile(b, m):
                if m == QK_ORDER[0]:
                    pe.wait_ge(s["attn_w_in"], 16 * 8)
                    h_ready("rms0", max(i for i in range(CHUNKS) if chunk("rms0", i)[0] == b))
                w, r = divmod(m, C * HALVES)
                f, half = divmod(r, HALVES)
                product(take(pe, first["qk", b, m]),
                        [(qk_w[:, w, c, f * P:(f + 1) * P], h[:, c, b, tok(half)]) for c in range(C)])\
                    .then_inc(s["tile_full"], 1)

            def v_tile(b, kt):
                product(take(pe, first["v", b, kt]),
                        [(h[:, c, b, kt * P:(kt + 1) * P], v_w[:, c].rearrange("p g e -> p (g e)"))
                         for c in range(C)]).then_inc(s["tile_full"], 1)

            def proj(q):
                b, half = divmod(q, HALVES)
                pe.wait_ge(s["attn_ready"], (b * HG + HG - 1) * HALVES + half + 1)
                for c in range(C):
                    product(take(pe, first["proj", q] + c),
                            [(proj_w[:, hg, c * P:(c + 1) * P], attnT[b][:, hg, tok(half)]) for hg in range(HG)])\
                        .then_inc(s["tile_full"], 1)

            def do(order):
                for kind, *at in order:
                    if kind == "mods":
                        modulation(*at)
                    if kind == "mean":
                        mean(*at)
                    if kind == "sum":
                        mean_square(*at)
                    if kind == "xs":
                        for f in range(NI):
                            in_path("xs", at[0], f, first["xs", at[0]] + f)
                    if kind == "zs":
                        in_path("zs", *at, first["zs", at[0], at[1]])
                    if kind == "dt":
                        x_proj(*at, first["dt", at[0], at[1]])
                    if kind == "bc":
                        x_proj(at[0], NI, first["bc", at[0]])
                    if kind == "out":
                        out_proj(*at)
                    if kind == "up":
                        up_tile(*at)
                    if kind == "down":
                        down_tile(*at)
                    if kind == "any key":
                        any_key()
                    if kind == "qk":
                        qk_tile(*at)
                    if kind == "v":
                        v_tile(*at)
                    if kind == "first pass":
                        for w in range(*at):
                            scores(w)
                    if kind == "proj":
                        proj(*at)

            pe.wait_ge(s["const_ready"], 10)
            do(START)
            for u in range(UNITS):
                base = u * DS

                def reduce(rhs, start, stop):
                    for f in range(NI):
                        if start and u:
                            pe.wait_ge(s["gated"], NI * (u - 1) + f + 1)
                        o = pe.matmul(psum[:, f, :], ident[:, :], rhs[:, f, :], start=start, stop=stop)
                        if stop and f < NI - 1:
                            o.then_inc(s["sum_ready"], 1)
                    return o

                def reduce_state(st, k, stop):
                    pe.wait_ge(s["prod_done"], st + (base + 5))
                    reduce(uh[:, k], False, stop).then_inc(s["reduce_done"], 1)

                pe.wait_ge(s["skip_ready"], NI * (u + 1))
                reduce(xs[:, u % 2], True, False)
                if u == UNITS - 1:
                    for g in range(DS // 4):
                        for k in range(4):
                            reduce_state(g * 4 + k, k, g * 4 + k == DS - 1)
                        if g < len(BESIDE):
                            do(BESIDE[g])
                    continue
                for g in range(SEGS):
                    last = g == SEGS - 1
                    with pe.Fori(g * ITERS, (g + 1) * ITERS - last) as i:
                        for k in range(4):
                            reduce_state(i * 4 + k, k, False)
                    if not last:
                        do(beside_unit(g, u))
                for k in range(4):
                    reduce_state(DS - 4 + k, k, k == 3)
            def scores(w):
                u, m = divmod(w, 4 * QT * HALVES)
                j, r = divmod(m, QT * HALVES)
                qt, kh = divmod(r, HALVES)
                if m == 0:
                    pe.wait_ge(s[f"stack_in_{u % STACKS}"], LOADS * (u // STACKS + 1))
                pe.matmul(take_side(pe, "scores", w), stack[u % STACKS][0:PLAIN, 0, j, qt * P:(qt + 1) * P],
                          stack[u % STACKS][0:PLAIN, 1, j, tok(kh)], start=True, stop=True)\
                  .then_inc(s["scores_full"], 1)

            def max_rows(half, u, j):
                pe.wait_ge(s["top_ready"], 4 * (u + 1))
                dst = take_side(pe, f"rows_{half}", 4 * u + j)
                for r in range(4):
                    o = pe.matmul(dst[ONE_ROW:ROWS, r * P:(r + 1) * P],
                                  top_parts[:, half * 4 + r, j, :], ident_b[:, :], start=True, stop=True)
                o.then_inc(s[f"rows_full_{half}"], 1)

            def scores2(v, m):
                u, qh = divmod(v, HALVES)
                kt, pair = divmod(m, 2)
                w = v * BLOCK + m
                if m < 2:
                    pe.wait_ge(s[f"rows_ready_{qh}"], 4 * (u + 1))
                for jj in range(2):
                    j = 2 * pair + jj
                    n = 2 * w + jj
                    if n >= 3:
                        pe.wait_ge(s["probs_ready"], n - 2)
                    pe.matmul(psum[:, n % 3, :], stack[u % STACKS][0:ROWS, 1, j, kt * P:(kt + 1) * P],
                              stack[u % STACKS][0:ROWS, 0, j, tok(qh)], start=True, stop=True)\
                      .then_inc(s["s2_full"], 1)

            def weigh_v(v, kt):
                b, hg = divmod(v // HALVES, HG)
                pe.wait_ge(s["probs_ready"], 2 * (v * BLOCK + 2 * kt + 2))
                if v and kt == 0:
                    pe.wait_ge(s["attn_copied"], v)
                for j in range(4):
                    o = pe.matmul(psum[32 * j:32 * j + 32, 4, :], v_aug[:, b, kt, hg, 32 * j:32 * j + 32],
                                  probs[:, 2 * (kt % 2) + j // 2, j % 2], start=kt == 0, stop=kt == QT - 1)
                o.then_inc(s["pv_done"], 1)

            def sums(v):
                pe.wait_ge(s["attn_copied"], v + 1)
                pe.matmul(take_side(pe, "sums", v), sum_sel[:, :], attn_sb[:, 0], start=True, stop=True)\
                  .then_inc(s["sums_full"], 1)

            do(LATE)
            pe.wait_ge(s["tile_free_act"], eaten(first["v", B - 1, QT - 1], "a"))
            pe.wait_ge(s["v_ready"], B)
            pe.wait_ge(s["scores_free"], ALONE)
            for j in range(4):
                max_rows(0, 0, j)
            for v in range(BLOCKS):
                for m in range(BLOCK):
                    scores2(v, m)
                    for w in scores_at(v, m):
                        scores(w)
                    if m % 2:
                        if m >= 3:
                            weigh_v(v, (m - 3) // 2)
                        elif v:
                            weigh_v(v - 1, QT - 1)
                    if m == SUMS_STEP and v:
                        sums(v - 1)
                    if rows_at(v, m):
                        max_rows(*rows_at(v, m))
            weigh_v(BLOCKS - 1, QT - 1)
            sums(BLOCKS - 1)
            pe.wait_ge(s["sums_copied"], BLOCKS)
            do(END)


def kernel(**inputs):
    import numpy as np
    import concourse.bacc as bacc
    from concourse.bass_utils import run_bass_kernel_spmd

    g = {k: np.asarray(v) for k, v in inputs.items()}
    l0, l1 = "L0_cond_", "L1_cond_"

    def lay(a):
        return np.ascontiguousarray(a)

    arrays = {
        "x": lay(g["x"].transpose(0, 2, 1)),
        "cond": lay(g["cond_1024"].T),
        "mask": lay(g["mask_BxS_ik0"]),
        "mamba_w": lay(g[l0 + "adaln_mamba_w"]), "mamba_b": lay(g[l0 + "adaln_mamba_b"]),
        "mlp_w": lay(g[l0 + "adaln_mlp_w"]), "mlp_b": lay(g[l0 + "adaln_mlp_b"]),
        "mlp_w1": lay(g[l0 + "mlp_w1"]), "mlp_w2": lay(g[l0 + "mlp_w2"]), "mlp_w3": lay(g[l0 + "mlp_w3"]),
        "norm_w": lay(g[l1 + "norm_w"]),
        "scale_w": lay(g[l1 + "scale_w"].T), "scale_b": lay(g[l1 + "scale_b"]),
        "shift_w": lay(g[l1 + "shift_w"].T), "shift_b": lay(g[l1 + "shift_b"]),
        "qkv_w": lay(g[l1 + "qkv_w"].T),
        "proj_w": lay(g[l1 + "proj_w"].T), "proj_b": lay(g[l1 + "proj_b"]),
        "up1_w": lay(g[l1 + "mlp_w1"].T), "up1_b": lay(g[l1 + "mlp_b1"]),
        "down1_w": lay(g[l1 + "mlp_w2"].T), "down1_b": lay(g[l1 + "mlp_b2"]),
    }
    for pre in ("fwd_", "bwd_"):
        for name in ("in_w", "xproj_w", "dt_bias", "A_log", "D", "out_w"):
            arrays[pre + name] = lay(g[l0 + pre + name])
    arrays = {k: lay(a.reshape(-1, P).T) if a.ndim == 1 else a for k, a in arrays.items()}

    nc = bacc.Bacc("TRN2", target_bir_lowering=False, num_devices=1)
    t = {k: nc.dram_tensor(f"in_{k}", a.shape, mybir.dt.from_np(a.dtype), kind="ExternalInput").ap()
         for k, a in arrays.items()}
    t["out"] = nc.dram_tensor("out_xT", (B, DM, L), mybir.dt.float32, kind="ExternalOutput").ap()
    build(nc, t)
    r = run_bass_kernel_spmd(nc, [{f"in_{k}": a for k, a in arrays.items()}], core_ids=[0])
    return lay(r.results[0]["out_xT"].transpose(0, 2, 1))
```
